# Optimizing a Trainium2 kernel written in Bass

```python
import numpy as np
import jax
import jax.numpy as jnp

def _softmax(x, axis=-1):
    return jax.nn.softmax(x, axis=axis)

def _gelu(x):
    return jax.nn.gelu(x, approximate=True)

def _silu(x):
    return jax.nn.silu(x)

def _sigmoid(x):
    return jax.nn.sigmoid(x)

def _layernorm(x, axis=-1, eps=1e-05):
    m = jnp.mean(x, axis=axis, keepdims=True)
    v = jnp.var(x, axis=axis, keepdims=True)
    return (x - m) / jnp.sqrt(v + eps)

def _scatter_add(tgt, idx, src, axis=0):
    return tgt.at[idx].add(src)

def _segment_sum(src, seg, n):
    return jax.ops.segment_sum(src, seg, n)
kernel_name = 'mk_gnn_resnorm_d4_gnn_r8_5e785b'

def setup_inputs(seed: int=0):
    np.random.seed(seed)
    _w = jnp.asarray

    def _rec_inputs():
        import jax
        import jax.numpy as jnp
        _gk = jax.random.key(seed)
        x = -0.0002928 + 1 * jax.random.normal(jax.random.fold_in(_gk, 1), (1024, 512), jnp.float32)
        src = jax.random.randint(jax.random.fold_in(_gk, 2), (32768,), 0, 1024, jnp.int32)
        dst = jnp.minimum((1024 * jax.random.uniform(jax.random.fold_in(_gk, 3), (32768,)) ** 2.0).astype(jnp.int32), 8191)
        _o = jnp.argsort(dst, stable=True)
        src = src[_o]
        dst = dst[_o]
        return (x, src, dst)
    x, src, dst = _rec_inputs()

    def _L0_gnn_setup():
        import jax, jax.numpy as jnp
        import numpy as np
        N_NODES = 1024
        N_EDGES = 32768
        D_IN = 512
        D_OUT = 512
        key = jax.random.key(seed)
        k1, k2, k3 = jax.random.split(key, 3)
        x = jax.random.normal(k1, (N_NODES, D_IN), dtype=jnp.float32)
        edge_index = jax.random.randint(k2, (2, N_EDGES), 0, N_NODES, dtype=jnp.int64)
        weight = jax.random.normal(k3, (D_IN, D_OUT), dtype=jnp.float32)
        bias = jnp.zeros((D_OUT,), dtype=jnp.float32)
        return {'x': x, 'edge_index': edge_index, 'weight': weight, 'bias': bias}
    _L0_gnn_all = _L0_gnn_setup()
    _L0_gnn_in = {k: v for k, v in _L0_gnn_all.items() if k in ('weight', 'bias')}
    del _L0_gnn_all

    def _L1_gnn_setup():
        import jax, jax.numpy as jnp
        import numpy as np
        N_NODES = 1250
        N_EDGES = 20000
        D_IN = 512
        D_HID = 512
        D_OUT = 512

        def _gcn_norm(edge_index, n_nodes):
            loop = jnp.arange(n_nodes, dtype=edge_index.dtype)
            src = jnp.concatenate([edge_index[0], loop])
            dst = jnp.concatenate([edge_index[1], loop])
            deg = jax.ops.segment_sum(jnp.ones_like(dst, dtype=jnp.float32), dst, num_segments=n_nodes)
            dinv = jnp.where(deg > 0, jax.lax.rsqrt(jnp.maximum(deg, 1.0)), 0.0)
            norm = dinv[src] * dinv[dst]
            return (src, dst, norm)

        def _gcn_conv(x, W, b, src, dst, norm, n_nodes):
            xw = x @ W
            msg = xw[src] * norm[:, None]
            out = jax.ops.segment_sum(msg, dst, num_segments=n_nodes)
            return out + b
        key = jax.random.key(seed)
        ks = jax.random.split(key, 8)
        x = jax.random.normal(ks[0], (N_NODES, D_IN), dtype=jnp.float32)
        edge_index = jax.random.randint(ks[1], (2, N_EDGES), 0, N_NODES, dtype=jnp.int64)

        def glorot(k, fan_in, fan_out):
            s = jnp.sqrt(6.0 / (fan_in + fan_out))
            return jax.random.uniform(k, (fan_in, fan_out), dtype=jnp.float32, minval=-s, maxval=s)
        W1 = glorot(ks[2], D_IN, D_HID)
        W2 = glorot(ks[3], D_HID, D_OUT)
        W3 = glorot(ks[4], D_OUT, D_OUT)
        b1 = jnp.zeros((D_HID,), jnp.float32)
        b2 = jnp.zeros((D_OUT,), jnp.float32)
        b3 = jnp.zeros((D_OUT,), jnp.float32)
        return {'x': x, 'edge_index': edge_index, 'W1': W1, 'b1': b1, 'W2': W2, 'b2': b2, 'W3': W3, 'b3': b3}
    _L1_gnn_all = _L1_gnn_setup()
    _L1_gnn_in = {k: v for k, v in _L1_gnn_all.items() if k in ('W1', 'b1', 'W2', 'b2', 'W3', 'b3')}
    del _L1_gnn_all

    def _L2_gnn_setup():
        import jax, jax.numpy as jnp
        import numpy as np
        NEG = -1000000.0
        key = jax.random.key(seed)
        ks = jax.random.split(key, 8)
        N, D_IN, D_Q, D_K, E = (1024, 512, 512, 512, 32768)
        s = 1.0 / np.sqrt(D_IN)
        return {'x': jax.random.normal(ks[0], (N, D_IN), dtype=jnp.float32), 'edge_index': jax.random.randint(ks[1], (2, E), 0, N, dtype=jnp.int64), 'Wq': jax.random.normal(ks[2], (D_IN, D_Q), dtype=jnp.float32) * s, 'bq': jax.random.normal(ks[3], (D_Q,), dtype=jnp.float32) * 0.01, 'Wk': jax.random.normal(ks[4], (D_IN, D_K), dtype=jnp.float32) * s, 'bk': jax.random.normal(ks[5], (D_K,), dtype=jnp.float32) * 0.01, 'Wv': jax.random.normal(ks[6], (D_IN, D_K), dtype=jnp.float32) * s, 'bv': jax.random.normal(ks[7], (D_K,), dtype=jnp.float32) * 0.01}
    _L2_gnn_all = _L2_gnn_setup()
    _L2_gnn_in = {k: v for k, v in _L2_gnn_all.items() if k in ('Wq', 'bq', 'Wk', 'bk', 'Wv', 'bv')}
    del _L2_gnn_all

    def _L3_gnn_setup():
        import jax, jax.numpy as jnp
        import numpy as np
        N_NODES = 1250

        def gcn_conv(x, edge_index, W, b):
            n = x.shape[0]
            h = x @ W
            loop = jnp.arange(n, dtype=edge_index.dtype)
            src = jnp.concatenate([edge_index[0], loop])
            dst = jnp.concatenate([edge_index[1], loop])
            ones = jnp.ones(src.shape[0], dtype=h.dtype)
            deg = jax.ops.segment_sum(ones, dst, num_segments=n)
            dis = jnp.where(deg > 0, jax.lax.rsqrt(deg), 0.0)
            norm = dis[src] * dis[dst]
            msg = h[src] * norm[:, None]
            out = jax.ops.segment_sum(msg, dst, num_segments=n)
            return out + b
        key = jax.random.key(seed)
        k1, k2, k3, k4, k5 = jax.random.split(key, 5)
        num_features, hidden, num_classes = (512, 512, 512)
        x = jax.random.normal(k1, (N_NODES, num_features), dtype=jnp.float32)
        edge_index = jax.random.randint(k2, (2, 20000), 0, N_NODES, dtype=jnp.int64)
        s1 = 1.0 / np.sqrt(num_features)
        s2 = 1.0 / np.sqrt(hidden)
        W1 = jax.random.uniform(k3, (num_features, hidden), jnp.float32, -s1, s1)
        b1 = jnp.zeros((hidden,), jnp.float32)
        W2 = jax.random.uniform(k4, (hidden, num_classes), jnp.float32, -s2, s2)
        b2 = jnp.zeros((num_classes,), jnp.float32)
        return {'x': x, 'edge_index': edge_index, 'W1': W1, 'b1': b1, 'W2': W2, 'b2': b2}
    _L3_gnn_all = _L3_gnn_setup()
    _L3_gnn_in = {k: v for k, v in _L3_gnn_all.items() if k in ('W1', 'b1', 'W2', 'b2')}
    del _L3_gnn_all
    return {'x': x, 'src': src, 'dst': dst, 'L0_gnn_weight': _L0_gnn_in['weight'], 'L0_gnn_bias': _L0_gnn_in['bias'], 'L1_gnn_W1': _L1_gnn_in['W1'], 'L1_gnn_b1': _L1_gnn_in['b1'], 'L1_gnn_W2': _L1_gnn_in['W2'], 'L1_gnn_b2': _L1_gnn_in['b2'], 'L1_gnn_W3': _L1_gnn_in['W3'], 'L1_gnn_b3': _L1_gnn_in['b3'], 'L2_gnn_Wq': _L2_gnn_in['Wq'], 'L2_gnn_bq': _L2_gnn_in['bq'], 'L2_gnn_Wk': _L2_gnn_in['Wk'], 'L2_gnn_bk': _L2_gnn_in['bk'], 'L2_gnn_Wv': _L2_gnn_in['Wv'], 'L2_gnn_bv': _L2_gnn_in['bv'], 'L3_gnn_W1': _L3_gnn_in['W1'], 'L3_gnn_b1': _L3_gnn_in['b1'], 'L3_gnn_W2': _L3_gnn_in['W2'], 'L3_gnn_b2': _L3_gnn_in['b2']}

def reference(x, src, dst, L0_gnn_weight, L0_gnn_bias, L1_gnn_W1, L1_gnn_b1, L1_gnn_W2, L1_gnn_b2, L1_gnn_W3, L1_gnn_b3, L2_gnn_Wq, L2_gnn_bq, L2_gnn_Wk, L2_gnn_bk, L2_gnn_Wv, L2_gnn_bv, L3_gnn_W1, L3_gnn_b1, L3_gnn_W2, L3_gnn_b2):
    import jax
    import jax.numpy as jnp

    def _L0_gnn_ref(x, edge_index, weight, bias):
        import jax, jax.numpy as jnp
        import numpy as np
        N_NODES = 1024
        N_EDGES = 32768
        D_IN = 512
        D_OUT = 512
        n = x.shape[0]
        adj = jnp.zeros((n, n), dtype=x.dtype)
        adj = adj.at[edge_index[0], edge_index[1]].set(1.0)
        adj = adj.at[edge_index[1], edge_index[0]].set(1.0)
        adj = adj + jnp.eye(n, dtype=x.dtype)
        deg = jnp.sum(adj, axis=1)
        dinv = 1.0 / jnp.sqrt(deg)
        adj = adj * dinv[:, None] * dinv[None, :]
        return adj @ (x @ weight) + bias

    def _L1_gnn_ref(x, edge_index, W1, b1, W2, b2, W3, b3):
        import jax, jax.numpy as jnp
        import numpy as np
        N_NODES = 1250
        N_EDGES = 20000
        D_IN = 512
        D_HID = 512
        D_OUT = 512

        def _gcn_norm(edge_index, n_nodes):
            loop = jnp.arange(n_nodes, dtype=edge_index.dtype)
            src = jnp.concatenate([edge_index[0], loop])
            dst = jnp.concatenate([edge_index[1], loop])
            deg = jax.ops.segment_sum(jnp.ones_like(dst, dtype=jnp.float32), dst, num_segments=n_nodes)
            dinv = jnp.where(deg > 0, jax.lax.rsqrt(jnp.maximum(deg, 1.0)), 0.0)
            norm = dinv[src] * dinv[dst]
            return (src, dst, norm)

        def _gcn_conv(x, W, b, src, dst, norm, n_nodes):
            xw = x @ W
            msg = xw[src] * norm[:, None]
            out = jax.ops.segment_sum(msg, dst, num_segments=n_nodes)
            return out + b
        n = x.shape[0]
        src, dst, norm = _gcn_norm(edge_index, n)
        h = _gcn_conv(x, W1, b1, src, dst, norm, n)
        h = _gcn_conv(h, W2, b2, src, dst, norm, n)
        h = _gcn_conv(h, W3, b3, src, dst, norm, n)
        return h

    def _L2_gnn_ref(x, edge_index, Wq, bq, Wk, bk, Wv, bv):
        import jax, jax.numpy as jnp
        import numpy as np
        NEG = -1000000.0
        q = x @ Wq + bq
        k = x @ Wk + bk
        v = x @ Wv + bv
        N = x.shape[0]
        adj = jnp.zeros((N, N), dtype=x.dtype).at[edge_index[0], edge_index[1]].set(1.0)
        a = q @ k.T / jnp.sqrt(jnp.asarray(q.shape[-1], dtype=x.dtype))
        a = a * adj + (1.0 - adj) * NEG
        attn = jax.nn.softmax(a, axis=-1)
        return attn @ v

    def _L3_gnn_ref(x, edge_index, W1, b1, W2, b2):
        import jax, jax.numpy as jnp
        import numpy as np
        N_NODES = 1250

        def gcn_conv(x, edge_index, W, b):
            n = x.shape[0]
            h = x @ W
            loop = jnp.arange(n, dtype=edge_index.dtype)
            src = jnp.concatenate([edge_index[0], loop])
            dst = jnp.concatenate([edge_index[1], loop])
            ones = jnp.ones(src.shape[0], dtype=h.dtype)
            deg = jax.ops.segment_sum(ones, dst, num_segments=n)
            dis = jnp.where(deg > 0, jax.lax.rsqrt(deg), 0.0)
            norm = dis[src] * dis[dst]
            msg = h[src] * norm[:, None]
            out = jax.ops.segment_sum(msg, dst, num_segments=n)
            return out + b
        h = jax.nn.relu(gcn_conv(x, edge_index, W1, b1))
        out = gcn_conv(h, edge_index, W2, b2)
        return out
    edge_index = jnp.stack([src, dst])
    x = _layernorm(x + _L0_gnn_ref(x, edge_index, L0_gnn_weight, L0_gnn_bias), axis=-1)
    x = _layernorm(x + _L1_gnn_ref(x, edge_index, L1_gnn_W1, L1_gnn_b1, L1_gnn_W2, L1_gnn_b2, L1_gnn_W3, L1_gnn_b3), axis=-1)
    x = _layernorm(x + _L2_gnn_ref(x, edge_index, L2_gnn_Wq, L2_gnn_bq, L2_gnn_Wk, L2_gnn_bk, L2_gnn_Wv, L2_gnn_bv), axis=-1)
    x = _layernorm(x + _L3_gnn_ref(x, edge_index, L3_gnn_W1, L3_gnn_b1, L3_gnn_W2, L3_gnn_b2), axis=-1)
    return x

_drawn_inputs = setup_inputs


def setup_inputs(seed=0):
    import zlib

    import numpy as np

    out = dict(_drawn_inputs(seed))
    spreads = {'L0_gnn_bias': (0.0, 0.1),
     'L1_gnn_b1': (0.0, 0.1),
     'L1_gnn_b2': (0.0, 0.1),
     'L1_gnn_b3': (0.0, 0.1),
     'L3_gnn_b1': (0.0, 0.1),
     'L3_gnn_b2': (0.0, 0.1)}
    factors = {'L2_gnn_bq': 29.93, 'L2_gnn_bk': 64.0, 'L2_gnn_bv': 6.245}
    for name, (base, spread) in spreads.items():
        noise = np.random.default_rng([zlib.crc32(name.encode()), seed]).standard_normal(out[name].shape)
        drawn = base * np.exp(spread * noise) if base else spread * noise
        out[name] = jnp.asarray(drawn.astype(out[name].dtype))
    for name, factor in factors.items():
        out[name] = (out[name] * factor).astype(out[name].dtype)
    return out
```

```python
from contextlib import ExitStack

import concourse.bass as bass
from concourse import mybir

ALU = mybir.AluOpType
ACT = mybir.ActivationFunctionType
AX = mybir.AxisListType
F32 = mybir.dt.float32
F32R = mybir.dt.float32r
BF16 = mybir.dt.bfloat16
I32 = mybir.dt.int32
I16 = mybir.dt.int16
U16 = mybir.dt.uint16

P = 128
EPS = 1e-5
NEG = -1000000.0
EXACT = 4096
FAR = 8192.0
CPG = 4
WIN = 40
BY_DVE = 2
EARLY = 16 * 128
SHARE = 1500
QUAD = 8
HALF = 4


def gnn_kernel(nc, x, src, dst, w0, b0, w1, b1, w2, b2, w3, b3, wq, bq, wk, bk, wv, bv, v1, c1, v2, c2, out):
    N, D = x.shape
    E = src.shape[0]
    NB = N // P
    FB = D // P
    G = E // (CPG * P)
    GE = CPG * P
    ROUNDS = (N + WIN - 1) // WIN
    KEYS = NB * WIN
    SCALE = float(D) ** -0.5
    assert D == 512 and NB == 2 * HALF and G % QUAD == 0 and KEYS <= 512 and G <= P

    with ExitStack() as ctx:
        place = [(nc.sbuf_base + 63) // 64 * 64]

        def region(size):
            start = place[0]
            place[0] += (size + 31) // 32 * 32
            assert place[0] <= nc.sbuf_usable_end
            return start

        def at(name, start, shape, dt):
            return nc.alloc_sbuf_tensor_at(name, shape, dt, offset=start)

        def sb(name, shape, dt):
            size = {F32: 4, F32R: 4, I32: 4, BF16: 2, I16: 2, U16: 2}[dt]
            for n in shape[1:]:
                size *= n
            return at(name, region(size), shape, dt)

        def sem(name):
            return ctx.enter_context(nc.semaphore(name))

        W = D * FB * 4
        adj = sb("adj", [P, NB, N], F32R)
        count = sb("count", [P, NB, N + WIN], U16)
        xs = sb("xs", [P, NB, D], F32)
        wfold = sb("wfold", [P, FB, D], F32)
        mfold = sb("mfold", [P, FB, D], F32)

        r1 = region(4 * W)
        x0t = at("x0t", r1, [P, FB, N], F32)
        w0_sb = at("w0_sb", r1 + 2 * W, [P, FB, D], F32)
        wqt = at("wqt", r1 + 3 * W, [P, FB, D], F32)
        sym = at("sym", r1, [P, NB, N], F32R)
        rest_l1 = at("rest_l1", r1, [P, NB, N], F32R)
        v1_sb = at("v1_sb", r1, [P, FB, D], F32)
        v2_sb = at("v2_sb", r1 + W, [P, FB, D], F32)
        xt = at("xt", r1 + 2 * W, [P, FB, N], F32)
        gt3 = at("gt3", r1 + 2 * W, [P, FB, N], F32)

        r2 = region(4 * W)
        wq_sb = at("wq_sb", r2, [P, FB, D], F32)
        wk_sb = at("wk_sb", r2 + W, [P, FB, D], F32)
        wkt = at("wkt", r2 + 2 * W, [P, FB, D], F32)
        w2_sb = at("w2_sb", r2 + 3 * W, [P, FB, D], F32)
        w3_sb = at("w3_sb", r2, [P, FB, D], F32)
        w1_sb = at("w1_sb", r2 + W, [P, FB, D], F32)
        w2t = at("w2t", r2 + 2 * W, [P, FB, D], F32)
        w1t = at("w1t", r2 + 2 * W, [P, FB, D], F32)
        w23 = at("w23", r2 + 3 * W, [P, FB, D], F32)
        ya = (at("ya_hi", r2, [P, NB, D], F32R), at("ya_lo", r2 + 2 * W, [P, NB, D], F32R))
        gt1 = at("gt1", r2, [P, FB, N], F32)
        score = at("score", r2, [P, 2, N], F32)
        away = at("away", r2 + 2 * N * 4, [P, 2, N], F32)
        probt = at("probt", r2 + 4 * N * 4, [P, 2, NB, P], F32)
        mask = at("mask", r2 + 6 * N * 4, [P, 2, N], BF16)

        r3 = region(4 * W)
        xw = at("xw", r3, [P, NB, D], F32)
        edge_rows = at("edge_rows", r3 + 2 * W, [G, 2, GE], I32)
        bits = at("bits", r3 + 2 * W + 4096, [G, 2, GE], I32)
        key_rows = at("key_rows", r3 + 2 * W + 8192, [G, 3, GE], F32)
        keyed = at("keyed", r3 + 2 * W, [P, 3, CPG * G], F32)
        link = at("link", r3 + 2 * W, [P, NB, N], BF16)
        yb = (at("yb_hi", r3, [P, NB, D], F32R), at("yb_lo", r3 + 2 * W, [P, NB, D], F32R))
        vv = at("vv", r3, [P, NB, D], F32)
        tt = at("tt", r3 + 2 * W, [P, FB, N], F32)
        rest_l3 = at("rest_l3", r3, [P, NB, N], F32R)

        r4 = region(W)
        hot_lo = at("hot_lo", r4, [P, 2 * CPG, P], BF16)
        hot_key = at("hot_key", r4 + 2 * CPG * P * 2, [P, 2 * CPG, KEYS], BF16)
        apart = at("apart", r3 + 2 * W + 8192, [P, 2, CPG - BY_DVE, P], BF16)
        wv_sb = at("wv_sb", r4, [P, FB, D], F32)
        hidden = at("hidden", r4, [P, 4, D], F32)

        edge_key = sb("edge_key", [P, 3, CPG * G], F32)
        bias0 = sb("bias0", [P, D], F32)
        bias3 = sb("bias3", [P, D], F32)
        biasv = sb("biasv", [P, D], F32)
        biasc1 = sb("biasc1", [P, D], F32)
        biasc2 = bias0
        fold1 = sb("fold1", [P, D], F32)
        fold2 = sb("fold2", [P, D], F32)
        urow = sb("urow", [P, D], F32)

        ident = sb("ident", [P, P], F32)
        identb = sb("identb", [P, P], BF16)
        ones = sb("ones", [P, P], F32)
        ones2 = sb("ones2", [P, 2], F32R)
        col_lo = sb("col_lo", [P, P], I16)
        col_key = sb("col_key", [P, KEYS], I16)
        span_at = sb("span_at", [P, ROUNDS], F32)
        bcol = sb("bcol", [P, 4, FB], F32)
        brow = sb("brow", [4 * FB, P], F32)
        bqb = sb("bqb", [P, FB], F32)
        group_lim = sb("group_lim", [G, 4], F32)
        group_dia = sb("group_dia", [G, 2, G], F32)
        group_row = sb("group_row", [P, 2, G], F32)
        base_at = sb("base_at", [1, G], I32)
        rounds_f = sb("rounds_f", [P, ROUNDS + 2], F32)
        flags = sb("flags", [1, 8], I32)
        shift = sb("shift", [P, 1], F32)
        tb = sb("tb", [P, FB], F32)
        c0 = sb("c0", [P, FB + 1], F32)
        degs = sb("degs", [P, 2, NB], F32)
        degmax = sb("degmax", [P, 2], F32)
        dinv = sb("dinv", [P, 3, NB], F32)
        mhalf = sb("mhalf", [P, NB], F32)
        ysum = sb("ysum", [P, NB, 2], F32R)
        avec = sb("avec", [P, 4, NB], F32)
        stats = sb("stats", [P, 6], F32)
        mv = sb("mv", [P, NB, 2], F32)
        veps = sb("veps", [P, NB], F32)
        rstd = sb("rstd", [P, NB], F32)
        rr = sb("rr", [P, NB], F32)
        peak = sb("peak", [P, 2, NB], F32)
        esum = sb("esum", [P, 2, NB], F32)

        bank = ctx.enter_context(nc.psum_tensor("bank", [P, 8, 512], F32))

        edges_in = sem("edges_in")
        x_in = [sem("x_in_low"), sem("x_in_high")]
        w_in = {k: sem("w_in_" + k) for k in ("q", "k", "0", "2", "3", "1", "v", "v1", "v2")}
        cols_in, rows_in = sem("cols_in"), sem("rows_in")
        const_set = sem("const_set")
        dve_set = sem("dve_set")
        pool_set = sem("pool_set")
        rows_set = sem("rows_set")
        rows_turned = sem("rows_turned")
        rounds_set = sem("rounds_set")
        round_set = sem("round_set")
        hot_set = sem("hot_set")
        apart_set = sem("apart_set")
        act_hot_set = sem("act_hot_set")
        win_summed = sem("win_summed")
        win_added = sem("win_added")
        counted = sem("counted")
        bqb_set = sem("bqb_set")
        unit_done = sem("unit_done")
        unit_out = sem("unit_out")
        link_set = sem("link_set")
        link_turned = sem("link_turned")
        sym_max = sem("sym_max")
        sym_set = sem("sym_set")
        adj_copied = sem("adj_copied")
        adj_set = sem("adj_set")
        deg0_set, dinv0_set = sem("deg0_set"), sem("dinv0_set")
        deg_summed, deg_out = sem("deg_summed"), sem("deg_out")
        degmax_set, degmax_all = sem("degmax_set"), sem("degmax_all")
        big_set = sem("big_set")
        rest_set = sem("rest_set")
        rest_part = sem("rest_part")
        rest_summed = sem("rest_summed")
        rest_added = sem("rest_added")
        deg_set, dinv_set = sem("deg_set"), sem("dinv_set")
        avec_split, avec_summed = sem("avec_split"), sem("avec_summed")
        avec_out = sem("avec_out")
        hi_set, lo_set = sem("hi_set"), sem("lo_set")
        hs_done = sem("hs_done")
        act_out, dve_out = sem("act_out"), sem("dve_out")
        var_set, rstd_set = sem("var_set"), sem("rstd_set")
        normed = sem("normed")
        biased = sem("biased")
        masks_set = sem("masks_set")
        scored = sem("scored")
        score_out = sem("score_out")
        peak_set = sem("peak_set")
        probs_set = sem("probs_set")
        probs_turned = sem("probs_turned")
        probt_set = sem("probt_set")
        mixed = sem("mixed")
        mixed_out = sem("mixed_out")
        stored = sem("stored")

        UNITS = [("xT", f, h) for h in range(2) for f in range(FB)]
        UNITS += [(kind, f, 0) for kind in ("wqT", "wkT") for f in range(FB)] + [("bT", 0, 0)]
        UNITS += [("m", f, 0) for f in range(FB)] + [("tb", 0, 0), ("u", 0, 0)]
        UNITS += [("xw", j, 0) for j in range(NB)]
        UNITS += [(kind, f, 0) for kind in ("w2T", "w23") for f in range(FB)] + [("g1", 0, 0)]
        UNITS += [(kind, f, 0) for kind in ("w1T", "wf") for f in range(FB)] + [("g2", 0, 0)]
        NU = len(UNITS)
        upto = {kind: n + 1 for n, (kind, _, _) in enumerate(UNITS)}
        def weight_of(m):
            kind = UNITS[m // 4][0]
            return {"T": P, "b": D // 2}.get(kind[-1], FB * P * 2)
        pieces = {}
        n, credit = 0, EARLY
        for g in range(-1, G):
            m = n
            while credit > 0 and m < 4 * NU:
                credit -= weight_of(m)
                m += 1
            pieces[g] = (n, m)
            n = m
            credit = min(credit, 0) + SHARE
        ALONG = n
        UA = n // 4

        WHO = "DD" "LL" "LL" "AA" "DD" "A" "D" "A" "A" "D" "A" "AA" "DD" "AA" "DD"
        def freed(s, b):
            who = WHO[s]
            n = HALF * WHO[:s].count(who) + b + 1
            if who == "L":
                return lo_set, 2 * NB + n
            return (act_out if who == "A" else dve_out), n

        block = ctx.enter_context(nc.Block())

        def wview(w):
            return w.rearrange("(c p) n -> p c n", p=P)

        @block.sync
        def _(sp):
            sp.dma_start(edge_rows[:, 0, :], dst.rearrange("(g e) -> g e", e=GE)).then_inc(edges_in, 16)
            sp.dma_start(edge_rows[:, 1, :], src.rearrange("(g e) -> g e", e=GE)).then_inc(edges_in, 16)
            for h in range(2):
                sp.dma_start(xs[:, HALF * h:HALF * (h + 1), :],
                             x[h * D:(h + 1) * D, :].rearrange("(b p) d -> p b d", p=P)).then_inc(x_in[h], 16)
            sp.dma_start(wq_sb[:], wview(wq)).then_inc(w_in["q"], 16)
            sp.dma_start(wk_sb[:], wview(wk)).then_inc(w_in["k"], 16)
            for n, b in enumerate((bq, bk, b1, b2)):
                sp.dma_start(brow[n * FB:(n + 1) * FB, :], b.rearrange("(c p) -> c p", p=P)).then_inc(cols_in, 16)
            sp.dma_start(w0_sb[:], wview(w0)).then_inc(w_in["0"], 16)
            for t, b in ((bias0, b0), (bias3, b3), (biasv, bv), (biasc1, c1)):
                sp.dma_start(t[:], b.partition_broadcast(P)).then_inc(rows_in, 16)
            sp.dma_start(w2_sb[:], wview(w2)).then_inc(w_in["2"], 16)
            sp.wait_ge(unit_done, upto["u"])
            sp.dma_start(w3_sb[:], wview(w3)).then_inc(w_in["3"], 16)
            sp.dma_start(w1_sb[:], wview(w1)).then_inc(w_in["1"], 16)
            sp.wait_ge(counted, 1)
            sp.dma_start(wv_sb[:], wview(wv)).then_inc(w_in["v"], 16)
            sp.wait_ge(hs_done, HALF * 8)
            sp.dma_start(v1_sb[:], wview(v1)).then_inc(w_in["v1"], 16)
            sp.dma_start(v2_sb[:], wview(v2)).then_inc(w_in["v2"], 16)
            sp.dma_start(biasc2[:], c2.partition_broadcast(P)).then_inc(rows_in, 16)
            for j in range(NB):
                sp.wait_ge(normed, 3 * NB + j + 1)
                sp.dma_start(out[j * P:(j + 1) * P, :], xs[:, j, :]).then_inc(stored, 16)
            sp.wait_ge(stored, 16 * NB)

        @block.gpsimd
        def _(pool):
            chain = [0]

            def then(ins):
                chain[0] += 1
                ins.then_inc(pool_set, 1)
                pool.wait_ge(pool_set, chain[0])

            then(nc.gpsimd.memset(ident[:], 0.0))
            then(nc.gpsimd.affine_select(out=ident[:], in_=ident[:], compare_op=ALU.not_equal, fill=1.0,
                                         base=0, pattern=[[-1, P]], channel_multiplier=1))
            nc.gpsimd.tensor_copy(identb[:], ident[:])
            nc.gpsimd.iota(span_at[:], pattern=[[WIN, ROUNDS]], base=0, channel_multiplier=0,
                           allow_small_or_imprecise_dtypes=True)
            nc.gpsimd.memset(ones[:], 1.0).then_inc(const_set, 1)
            nc.gpsimd.iota(col_lo[:], pattern=[[1, P]], base=0, channel_multiplier=0,
                           allow_small_or_imprecise_dtypes=True)
            nc.gpsimd.iota(col_key[:], pattern=[[1, KEYS]], base=0, channel_multiplier=0,
                           allow_small_or_imprecise_dtypes=True)
            nc.gpsimd.memset(mhalf[:], -0.5)
            nc.gpsimd.memset(ones2[:].bitcast(F32), 1.0).then_inc(const_set, 1)
            nc.gpsimd.memset(count[:].bitcast(F32), 0.0).then_inc(const_set, 1)
            pool.wait_ge(unit_out, upto["bT"])
            nc.gpsimd.tensor_tensor(bqb[:], bcol[:, 0, :], bcol[:, 1, :], ALU.mult).then_inc(bqb_set, 1)
            pool.wait_ge(rows_in, 16 * 4)
            pool.wait_ge(unit_done, upto["xT"])
            for j in range(NB):
                nc.gpsimd.tensor_tensor(xs[:, j, :], xs[:, j, :], bias0[:], ALU.add).then_inc(biased, 1)
            pool.wait_ge(deg0_set, 1)
            nc.gpsimd.tensor_tensor(dinv[:, 0, :], degs[:, 0, :], mhalf[:], ALU.pow).then_inc(dinv0_set, 1)
            pool.wait_ge(degmax_set, 1)
            nc.gpsimd.partition_all_reduce(degmax[:, 1:2], degmax[:, 0:1], P,
                                           bass.bass_isa.ReduceOp.max).then_inc(degmax_all, 1)

            def inverse_roots(first, last):
                for n in range(first, last):
                    j = n % NB
                    pool.wait_ge(var_set, n + 1)
                    nc.gpsimd.tensor_tensor(rstd[:, j:j + 1], veps[:, j:j + 1], mhalf[:, j:j + 1],
                                            ALU.pow).then_inc(rstd_set, 1)

            inverse_roots(0, HALF)
            pool.wait_ge(deg_set, 1)
            then(nc.gpsimd.tensor_tensor(dinv[:, 1, :], degs[:, 1, :], mhalf[:], ALU.pow))
            nc.gpsimd.tensor_tensor(dinv[:, 2, :], dinv[:, 1, :], dinv[:, 1, :], ALU.mult).then_inc(dinv_set, 1)
            inverse_roots(HALF, NB)
            for j in range(NB):
                pool.wait_ge(lo_set, NB + j + 1)
                nc.gpsimd.tensor_tensor(xs[:, j, :], xs[:, j, :], bias3[:], ALU.add).then_inc(biased, 1)
            inverse_roots(NB, 2 * NB)
            pool.wait_ge(*freed(10, 0))
            for i in range(NB):
                if i >= 2:
                    pool.wait_ge(peak_set, i - 1)
                then(nc.gpsimd.tensor_scalar(mask[:, i % 2, :], count[:, i, 0:N], 1.0, None, ALU.min))
                nc.gpsimd.tensor_scalar(away[:, i % 2, :], mask[:, i % 2, :], -1.0, -NEG,
                                        ALU.add, ALU.mult).then_inc(masks_set, 1)
                if i >= 2:
                    inverse_roots(2 * NB + i - 2, 2 * NB + i - 1)
            inverse_roots(3 * NB - 2, 3 * NB)
            pool.wait_ge(rows_in, 16 * 5)
            for j in range(NB):
                pool.wait_ge(lo_set, 4 * NB + j + 1)
                nc.gpsimd.tensor_tensor(xs[:, j, :], xs[:, j, :], biasc2[:], ALU.add).then_inc(biased, 1)
            inverse_roots(3 * NB, 4 * NB)

        @block.tensor
        def _(pe):
            def piece(m):
                n, k = m // 4, m % 4
                kind, f, h = UNITS[n]
                to = bank[:, 4 + n % 4, :]
                if k == 0 and n >= 4:
                    pe.wait_ge(unit_out, n - 3)
                first, last = k == 0, k == FB - 1
                cols = slice(k * P, (k + 1) * P)
                rows = slice(f * P, (f + 1) * P)
                if kind == "xT":
                    pe.wait_ge(x_in[h], 16)
                    mm = pe.transpose(to[:, cols], xs[:, 4 * h + k, rows], ident[:])
                elif kind in ("wqT", "wkT", "w2T", "w1T"):
                    w = {"wqT": wq_sb, "wkT": wk_sb, "w2T": w2_sb, "w1T": w1_sb}[kind]
                    pe.wait_ge(w_in[kind[1]], 16)
                    mm = pe.transpose(to[:, cols], w[:, k, rows], ident[:])
                elif kind == "bT":
                    if not last:
                        return
                    pe.wait_ge(cols_in, 16 * 4)
                    mm = pe.transpose(to[:, 0:4 * FB], brow[:], ident[0:4 * FB, 0:4 * FB])
                elif kind == "m":
                    pe.wait_ge(unit_out, upto["wkT"])
                    mm = pe.matmul(to, wqt[:, k, rows], wkt[:, k, :], start=first, stop=last)
                elif kind == "tb":
                    pe.wait_ge(unit_out, upto["bT"])
                    for c in range(FB):
                        mm = pe.matmul(to[:, k:k + 1], wkt[:, c, cols], bcol[:, 0, c:c + 1],
                                       start=c == 0, stop=c == FB - 1)
                    if last:
                        pe.wait_ge(bqb_set, 1)
                        mm = pe.matmul(to[:, FB:2 * FB], ones[:], bqb[:], start=True, stop=True)
                elif kind in ("u", "g1", "g2"):
                    pe.wait_ge(unit_out, upto["bT"])
                    n_b, w = {"u": (1, wqt), "g1": (3, w3_sb), "g2": (2, w23)}[kind]
                    if kind == "g2":
                        pe.wait_ge(unit_out, upto["w23"])
                    mm = pe.matmul(to, bcol[:, n_b, k:k + 1].to_broadcast([P, P]), w[:, k, :],
                                   start=first, stop=last)
                elif kind == "xw":
                    pe.wait_ge(w_in["0"], 16)
                    pe.wait_ge(unit_out, upto["xT"])
                    mm = pe.matmul(to, x0t[:, k, rows], w0_sb[:, k, :], start=first, stop=last)
                elif kind == "w23":
                    pe.wait_ge(w_in["3"], 16)
                    pe.wait_ge(unit_out, upto["w2T"])
                    mm = pe.matmul(to, w2t[:, k, rows], w3_sb[:, k, :], start=first, stop=last)
                elif kind == "wf":
                    pe.wait_ge(unit_out, upto["w1T"])
                    mm = pe.matmul(to, w1t[:, k, rows], w23[:, k, :], start=first, stop=last)
                if last:
                    mm.then_inc(unit_done, 1)

            pe.wait_ge(const_set, 1)
            pe.wait_ge(rows_set, 1)
            pe.matmul(bank[:, 0, 0:2 * G], ones[0:G, :], group_dia[:].rearrange("g a b -> g (a b)"),
                      start=True, stop=True).then_inc(rows_turned, 1)
            pe.wait_ge(rows_set, 2)
            for n in range(3):
                for c in range(CPG):
                    at_col = ((n % 2) * CPG + c) * G
                    mm = pe.transpose(bank[:, 2 + n // 2, at_col:at_col + G],
                                      key_rows[:, n, c * P:(c + 1) * P], ident[0:G, 0:G])
            mm.then_inc(rows_turned, 1)

            def chunk(at_hot, at_bank, c):
                return pe.matmul(bank[:, at_bank, 0:KEYS], hot_lo[:, at_hot, :], hot_key[:, at_hot, :],
                                 start=c == 0, stop=c == CPG - 1)

            for m in range(*pieces[-1]):
                piece(m)
            for g in range(G):
                pe.wait_ge(win_added, g + 1)
                for c in range(CPG):
                    pe.wait_ge(hot_set, CPG * g + c + 1)
                    if c == BY_DVE:
                        pe.wait_ge(act_hot_set, g + 1)
                    mm = chunk((g % 2) * CPG + c, g % 2, c)
                mm.then_inc(win_summed, 1)
                for m in range(*pieces[g]):
                    piece(m)
            pe.wait_ge(rounds_set, 1)
            rounds = pe.value_load(flags[0:1, 0:1], min_val=1, max_val=ROUNDS)
            with pe.If(rounds > 1):
                with pe.Fori(1, rounds) as r:
                    with pe.Fori(0, G // QUAD) as q:
                        for n in range(QUAD):
                            pe.wait_ge(win_added, r * G + q * QUAD + (n + 1))
                            for c in range(CPG):
                                pe.wait_ge(hot_set, (r * G + q * QUAD) * CPG + (n * CPG + c + 1))
                                if c == BY_DVE:
                                    pe.wait_ge(act_hot_set, r * G + q * QUAD + (n + 1))
                                mm = chunk((n % 2) * CPG + c, n % 2, c)
                            mm.then_inc(win_summed, 1)
                pe.nop()

            def turn_links(h):
                if h == 0:
                    pe.wait_ge(link_set, NB)
                if h >= 2:
                    pe.wait_ge(sym_max, h - 1)
                to = bank[:, h % 2, :].bitcast(BF16)
                for j in range(NB):
                    mm = pe.transpose(to[:, j * P:(j + 1) * P], link[:, j, h * P:(h + 1) * P], identb[:])
                mm.then_inc(link_turned, 1)

            left = 4 * NU - ALONG
            for h in range(NB):
                for m in range(ALONG + left * h // NB, ALONG + left * (h + 1) // NB):
                    piece(m)
                turn_links(h)

            def rows_step(s, mat, y, lo_from, more=None):
                for k in range(NB):
                    pe.wait_ge(lo_set, lo_from + k + 1)
                    if s < 2:
                        pe.wait_ge(sym_set, k + 1)
                    for b in range(HALF):
                        j = HALF * (s % 2) + b
                        if k == 0:
                            bank_free(s, b)
                        to = bank[:, HALF * (s % 2) + b, :]
                        for m in [mat] + ([more] if more is not None else []):
                            for part in range(2):
                                mm = pe.matmul(to, m[:, k, j * P:(j + 1) * P], y[part][:, k, :],
                                               start=k == 0 and part == 0 and m is mat,
                                               stop=k == NB - 1 and part == 1 and (more is None or m is more))
                        if k == NB - 1:
                            mm.then_inc(hs_done, 1)

            def cols_step(s, mat, y, lo_from, more=None):
                half = slice((s % 2) * D, (s % 2 + 1) * D)
                for k in range(NB):
                    pe.wait_ge(lo_set, lo_from + k + 1)
                    for f in range(FB):
                        if k == 0:
                            bank_free(s, f)
                        to = bank[:, HALF * (s % 2) + f, :]
                        for m in [mat] + ([more] if more is not None else []):
                            for part in range(2):
                                mm = pe.matmul(to, y[part][:, k, f * P:(f + 1) * P], m[:, k, half],
                                               start=k == 0 and part == 0 and m is mat,
                                               stop=k == NB - 1 and part == 1 and (more is None or m is more))
                        if k == NB - 1:
                            mm.then_inc(hs_done, 1)

            def bank_free(s, b):
                if s == 0:
                    if b == 0:
                        pe.wait_ge(sym_max, NB)
                elif s == 1:
                    if b == 0:
                        pe.wait_ge(unit_out, NU)
                        pe.wait_ge(deg_out, 1)
                elif s == 16:
                    if b == 0:
                        pe.wait_ge(score_out, NB)
                elif s == 17:
                    if b == 0:
                        pe.wait_ge(probt_set, NB)
                        pe.wait_ge(mixed_out, NB)
                else:
                    pe.wait_ge(*freed(s - 2, b))

            def weight_step(s, half, g, w, ready):
                pe.wait_ge(*ready)
                for b in range(HALF):
                    bank_free(s, b)
                    j = HALF * half + b
                    for k in range(FB):
                        mm = pe.matmul(bank[:, HALF * (s % 2) + b, :], g[:, k, j * P:(j + 1) * P], w[:, k, :],
                                       start=k == 0, stop=k == FB - 1)
                    mm.then_inc(hs_done, 1)

            def sums(to, mats, rhs):
                for j in range(NB):
                    for k in range(NB):
                        for m in mats:
                            mm = pe.matmul(to[:, 2 * j:2 * j + 2], m[:, k, j * P:(j + 1) * P], rhs(k),
                                           start=k == 0 and m is mats[0], stop=k == NB - 1 and m is mats[-1])
                return mm

            rows_step(0, sym, ya, 0)
            pe.wait_ge(adj_set, NB)
            pe.wait_ge(const_set, 2)
            pe.wait_ge(unit_out, NU)
            sums(bank[:, 4, :], [adj], lambda k: ones2[:]).then_inc(deg_summed, 1)
            rows_step(1, sym, ya, 0)

            pe.wait_ge(big_set, 1)
            big = pe.value_load(flags[0:1, 4:5], min_val=0, max_val=1)

            def vectors(mats):
                for n in range(2):
                    pe.wait_ge(*freed(0, n))
                    pe.wait_ge(avec_split, n + 1)
                    sums(bank[:, n, :], mats, lambda k: ysum[:, k, :]).then_inc(avec_summed, 1)

            def layer1(mats):
                more = mats[1] if len(mats) > 1 else None
                vectors(mats)
                pe.wait_ge(avec_out, 2)
                for s in (2, 3):
                    rows_step(s, adj, yb, NB, more)
                for s in (4, 5):
                    rows_step(s, adj, ya, 2 * NB, more)
                for s in (6, 7):
                    cols_step(s, adj, yb, 3 * NB, more)

            with pe.If(big > 0):
                pe.wait_ge(rest_set, 1)
                pe.wait_ge(*freed(0, 0))
                sums(bank[:, 0, :], [rest_l1], lambda k: ones2[:]).then_inc(rest_summed, 1)
                layer1([adj, rest_l1])
            with pe.Else():
                layer1([adj])
            for half in range(2):
                weight_step(8 + half, half, gt1, wfold, freed(6 + half, 3))

            pe.wait_ge(w_in["v"], 16)
            for half in range(2):
                s = 10 + 3 * half
                for f in range(FB):
                    bank_free(s, f)
                    for b in range(HALF):
                        j = HALF * half + b
                        pe.wait_ge(normed, NB + j + 1)
                        mm = pe.transpose(bank[:, HALF * (s % 2) + f, b * P:(b + 1) * P],
                                          xs[:, j, f * P:(f + 1) * P], ident[:])
                    mm.then_inc(hs_done, 1)
                weight_step(s + 1, half, xt, wv_sb, freed(s, 3))
                for f in range(FB):
                    bank_free(s + 2, f)
                    for k in range(FB):
                        mm = pe.matmul(bank[:, HALF * (s % 2) + f, :], mfold[:, k, f * P:(f + 1) * P],
                                       xt[:, k, half * D:(half + 1) * D], start=k == 0, stop=k == FB - 1)
                    mm.then_inc(hs_done, 1)

            def scores(i):
                pe.wait_ge(*freed(12 if i < HALF else 15, 3))
                if i >= 2:
                    pe.wait_ge(score_out, i - 1)
                for c in range(2):
                    if i < 2:
                        pe.wait_ge(*freed(14, 2 * i + c))
                    for k in range(FB):
                        mm = pe.matmul(bank[:, 2 * (i % 2) + c, :], tt[:, k, i * P:(i + 1) * P],
                                       xt[:, k, c * D:(c + 1) * D], start=k == 0, stop=k == FB - 1)
                mm.then_inc(scored, 1)

            def turn_probs(i):
                pe.wait_ge(probs_set, i + 1)
                pe.wait_ge(*(freed(15, 1) if i == 0 else (probt_set, i)))
                for j in range(NB):
                    mm = pe.transpose(bank[:, 4 + j // 4, (j % 4) * P:(j % 4 + 1) * P],
                                      score[:, i % 2, j * P:(j + 1) * P], ident[:])
                mm.then_inc(probs_turned, 1)

            def mix(i):
                pe.wait_ge(probt_set, i + 1)
                pe.wait_ge(*(freed(15, 2 + i) if i < 2 else (mixed_out, i - 1)))
                if i == 0:
                    pe.wait_ge(*freed(14, 3))
                for j in range(NB):
                    mm = pe.matmul(bank[:, 6 + i % 2, :], probt[:, i % 2, j, :], vv[:, j, :],
                                   start=j == 0, stop=j == NB - 1)
                mm.then_inc(mixed, 1)

            pe.wait_ge(*freed(13, 3))
            scores(0)
            for i in range(NB):
                if i + 1 < NB:
                    scores(i + 1)
                turn_probs(i)
                mix(i)

            def layer3(mats):
                more = mats[1] if len(mats) > 1 else None
                for n, w in enumerate((v1_sb, v2_sb)):
                    for half in range(2):
                        cols_step(16 + 4 * n + half, adj, ya, (4 + n) * NB, more)
                    pe.wait_ge(w_in["v1" if n == 0 else "v2"], 16)
                    for half in range(2):
                        weight_step(18 + 4 * n + half, half, gt3, w, freed(16 + 4 * n + half, 3))

            with pe.If(big > 0):
                pe.wait_ge(rest_set, 2)
                layer3([adj, rest_l3])
            with pe.Else():
                layer3([adj])

        @block.scalar
        def _(act):
            def copy_unit(n):
                kind, f, h = UNITS[n]
                at_bank = bank[:, 4 + n % 4, :]
                act.wait_ge(unit_done, n + 1)
                if kind == "w2T" and f == 0:
                    act.wait_ge(unit_done, upto["u"])
                if kind == "xT":
                    ins = nc.scalar.copy(x0t[:, f, h * D:(h + 1) * D], at_bank)
                elif kind == "bT":
                    ins = nc.scalar.copy(bcol[:].rearrange("p n c -> p (n c)"), at_bank[:, 0:4 * FB])
                elif kind == "m":
                    ins = nc.scalar.mul(mfold[:, f, :], at_bank, SCALE)
                elif kind == "tb":
                    nc.scalar.mul(tb[:], at_bank[:, 0:FB], SCALE)
                    ins = nc.scalar.mul(c0[:, 0:FB], at_bank[:, FB:2 * FB], SCALE)
                elif kind == "u":
                    ins = nc.scalar.mul(urow[:], at_bank, SCALE)
                else:
                    to = {"wqT": wqt, "wkT": wkt, "xw": xw, "w2T": w2t, "w23": w23, "w1T": w1t,
                          "wf": wfold, "g1": fold1, "g2": fold2}[kind]
                    ins = nc.scalar.copy(to[:, f, :] if kind[0] != "g" else to[:], at_bank)
                ins.then_inc(unit_out, 1)

            def low_one_hots(g, slot, before):
                for c in range(BY_DVE, CPG):
                    ins = nc.scalar.activation(apart[:, slot, c - BY_DVE, :], col_lo[:], ACT.Abs, scale=-1.0,
                                               bias=edge_key[:, 0, bass.ds(g + c * G, 1)])
                ins.then_inc(apart_set, 1)
                act.wait_ge(apart_set, before + 1)
                nc.scalar.activation(hot_lo[:, slot * CPG + BY_DVE:(slot + 1) * CPG, :], apart[:, slot], ACT.Relu,
                                     scale=-1.0, bias=ones[:, 0:1]).then_inc(act_hot_set, 1)

            act.wait_ge(const_set, 2)
            for n in range(pieces[-1][1] // 4):
                copy_unit(n)
            act.wait_ge(win_added, 1)
            for g in range(G):
                if g >= 2:
                    act.wait_ge(win_summed, g - 1)
                low_one_hots(g, g % 2, g)
                if g >= 2:
                    for n in range(pieces[g - 2][0] // 4, pieces[g - 2][1] // 4):
                        copy_unit(n)
            for n in range(pieces[G - 2][0] // 4, UA):
                copy_unit(n)
            act.wait_ge(rounds_set, 1)
            rounds = act.value_load(flags[0:1, 0:1], min_val=1, max_val=ROUNDS)
            with act.If(rounds > 1):
                with act.Fori(1, rounds) as r:
                    with act.Fori(0, G // QUAD) as q:
                        for n in range(QUAD):
                            act.wait_ge(win_summed, r * G + q * QUAD + (n - 1))
                            low_one_hots(q * QUAD + n, n % 2, r * G + q * QUAD + n)
                act.nop()
            act.wait_ge(counted, 1)
            for h in range(NB):
                nc.scalar.copy(adj[:, h, :], count[:, h, 0:N]).then_inc(adj_copied, 1)
            for n in range(UA, NU):
                copy_unit(n)

            act.wait_ge(dinv0_set, 1)
            act.wait_ge(unit_out, NU)
            for k in range(NB):
                nc.scalar.activation(ya[0][:, k, :], xw[:, k, :], ACT.Copy, scale=dinv[:, 0, k:k + 1]).then_inc(hi_set, 1)
            act.wait_ge(dinv_set, 1)
            for k in range(NB):
                act.wait_ge(normed, k + 1)
                nc.scalar.activation(yb[0][:, k, :], xs[:, k, :], ACT.Copy, scale=dinv[:, 1, k:k + 1]).then_inc(hi_set, 1)
            for n, y in ((0, ya), (1, yb)):
                for k in range(NB):
                    act.wait_ge(hs_done, (2 + 2 * n) * HALF + k + 1)
                    nc.scalar.activation(y[0][:, k, :], bank[:, k, :], ACT.Copy,
                                         scale=dinv[:, 2, k:k + 1]).then_inc(hi_set, 1)

            def copy_cols(s, half, to, bias=None):
                for f in range(FB):
                    act.wait_ge(hs_done, s * HALF + f + 1)
                    at_bank = bank[:, HALF * (s % 2) + f, :]
                    to_f = to[:, f, half * D:(half + 1) * D]
                    if bias is None:
                        nc.scalar.copy(to_f, at_bank).then_inc(act_out, 1)
                    else:
                        nc.scalar.activation(to_f, at_bank, ACT.Identity, bias=bias[:, f:f + 1]).then_inc(act_out, 1)

            copy_cols(6, 0, gt1)
            copy_cols(7, 1, gt1)
            for half in range(2):
                copy_cols(10 + 3 * half, half, xt)
                copy_cols(12 + 3 * half, half, tt, tb)
            for i in range(NB):
                act.wait_ge(peak_set, i + 1)
                nc.scalar.activation(score[:, i % 2, :], score[:, i % 2, :], ACT.Exp, bias=peak[:, 1, i:i + 1],
                                     accum_out=esum[:, 0, i:i + 1]).then_inc(probs_set, 1)
                act.wait_ge(probs_turned, i + 1)
                if i >= 2:
                    act.wait_ge(mixed, i - 1)
                nc.scalar.copy(probt[:, i % 2, :, :].rearrange("p j q -> p (j q)"),
                               bank[:, 4:6, :].rearrange("p a b -> p (a b)")).then_inc(probt_set, 1)
            act.wait_ge(mixed, NB)
            for k in range(NB):
                act.wait_ge(normed, 2 * NB + k + 1)
                nc.scalar.activation(ya[0][:, k, :], xs[:, k, :], ACT.Copy, scale=dinv[:, 1, k:k + 1]).then_inc(hi_set, 1)
            copy_cols(16, 0, gt3)
            copy_cols(17, 1, gt3)
            for k in range(NB):
                act.wait_ge(*freed(18 + k // HALF, k % HALF))
                nc.scalar.activation(ya[0][:, k, :], hidden[:, k % 4, :], ACT.Relu,
                                     scale=dinv[:, 1, k:k + 1]).then_inc(hi_set, 1)
            copy_cols(20, 0, gt3)
            copy_cols(21, 1, gt3)

        @block.vector
        def _(dve):
            V = nc.vector
            chain = [0]

            def then(ins):
                chain[0] += 1
                ins.then_inc(dve_set, 1)
                dve.wait_ge(dve_set, chain[0])

            dve.wait_ge(edges_in, 32)
            V.tensor_reduce(group_lim[:, 0:1], edge_rows[:, 0, :], AX.X, ALU.min)
            then(V.tensor_reduce(group_lim[:, 1:2], edge_rows[:, 0, :], AX.X, ALU.max))
            then(V.tensor_tensor(group_lim[:, 2:3], group_lim[:, 1:2], group_lim[:, 0:1], ALU.subtract))
            dve.wait_ge(const_set, 1)
            V.tensor_scalar(group_dia[:, 0, :], ident[0:G, 0:G], group_lim[:, 0:1], None, ALU.mult)
            V.tensor_scalar(group_dia[:, 1, :], ident[0:G, 0:G], group_lim[:, 2:3], None,
                            ALU.mult).then_inc(rows_set, 1)
            V.tensor_scalar(bits[:, 0, :], edge_rows[:, 1, :], P - 1, None, ALU.bitwise_and)
            then(V.tensor_scalar(bits[:, 1, :], edge_rows[:, 1, :], P.bit_length() - 1, None, ALU.arith_shift_right))
            V.tensor_copy(key_rows[:, 0, :], bits[:, 0, :])
            V.tensor_scalar(key_rows[:, 1, :], bits[:, 1, :], float(WIN), None, ALU.mult)
            V.tensor_scalar(key_rows[:, 2, :], edge_rows[:, 0, :], group_lim[:, 0:1], None,
                            ALU.subtract).then_inc(rows_set, 1)
            dve.wait_ge(rows_turned, 1)
            then(V.tensor_copy(group_row[:].rearrange("p a g -> p (a g)"), bank[:, 0, 0:2 * G]))
            then(V.tensor_reduce(rounds_f[:, ROUNDS:ROUNDS + 1], group_row[:, 1, :], AX.X, ALU.max))
            then(V.tensor_scalar(rounds_f[:, 0:ROUNDS], span_at[:], rounds_f[:, ROUNDS:ROUNDS + 1], None, ALU.is_le))
            then(V.tensor_reduce(rounds_f[:, ROUNDS + 1:ROUNDS + 2], rounds_f[:, 0:ROUNDS], AX.X, ALU.add))
            then(V.tensor_copy(flags[0:1, 0:1], rounds_f[0:1, ROUNDS + 1:ROUNDS + 2]))
            V.memset(shift[:], 0.0).then_inc(rounds_set, 1)
            dve.wait_ge(rounds_set, 1)
            dve.wait_ge(rows_turned, 2)
            V.tensor_copy(edge_key[:, 0:2, :].rearrange("p a g -> p (a g)"), bank[:, 2, :]).then_inc(win_added, 1)
            V.tensor_copy(edge_key[:, 2, :], bank[:, 3, 0:CPG * G]).then_inc(win_added, 1)
            dve.wait_ge(win_added, 2)
            dve.wait_ge(const_set, 3)
            rounds = dve.value_load(flags[0:1, 0:1], min_val=1, max_val=ROUNDS)

            def one_hots(g, slot, chunks=range(CPG)):
                for c in chunks:
                    if c < BY_DVE:
                        V.tensor_scalar(hot_lo[:, slot * CPG + c, :], col_lo[:],
                                        edge_key[:, 0, bass.ds(g + c * G, 1)], None, ALU.is_equal)
                    V.tensor_scalar(hot_key[:, slot * CPG + c, :], col_key[:],
                                    keyed[:, 0, bass.ds(g + c * G, 1)], None, ALU.is_equal).then_inc(hot_set, 1)

            def windows_at(g):
                _, values = nc.values_load_multi_w_load_instructions(
                    base_at[0:1, bass.ds(g, QUAD)], engines=[mybir.EngineType.DVE], min_val=0, max_val=N)
                return values

            def add_window(at_dst, seen, slot):
                dve.wait_ge(win_summed, seen + 1)
                dve.wait_ge(win_added, seen + 2)
                V.tensor_tensor(count[:, :, bass.ds(at_dst, WIN)],
                                bank[:, slot, 0:KEYS].rearrange("p (h d) -> p h d", h=NB),
                                count[:, :, bass.ds(at_dst, WIN)], ALU.add).then_inc(win_added, 1)

            SETUP = 8
            with dve.Fori(0, rounds) as r:
                def after(ins, n):
                    ins.then_inc(round_set, 1)
                    dve.wait_ge(round_set, r * SETUP + n)

                after(V.tensor_scalar(keyed[:, 1, :], edge_key[:, 2, :], shift[:], None, ALU.subtract), 1)
                after(V.tensor_scalar(keyed[:, 0, :], keyed[:, 1, :], 0.0, FAR, ALU.is_lt, ALU.mult), 2)
                after(V.tensor_scalar(keyed[:, 2, :], keyed[:, 1, :], float(WIN), FAR, ALU.is_ge, ALU.mult), 3)
                after(V.tensor_tensor(keyed[:, 0, :], keyed[:, 0, :], keyed[:, 2, :], ALU.add), 4)
                after(V.tensor_tensor(keyed[:, 0, :], keyed[:, 0, :], keyed[:, 1, :], ALU.add), 5)
                after(V.tensor_tensor(keyed[:, 0, :], keyed[:, 0, :], edge_key[:, 1, :], ALU.add), 6)
                after(V.tensor_scalar(base_at[:], group_row[0:1, 0, :], shift[0:1, :], float(N), ALU.add, ALU.min), 7)
                after(V.tensor_scalar(shift[:], shift[:], float(WIN), None, ALU.add), 8)
                one_hots(0, 0)
                with dve.Fori(0, G // QUAD - 1) as q:
                    places = windows_at(q * QUAD)
                    for n in range(QUAD):
                        one_hots(q * QUAD + (n + 1), (n + 1) % 2)
                        add_window(places[n], r * G + q * QUAD + n, n % 2)
                places = windows_at(G - QUAD)
                for n in range(G - QUAD, G):
                    if n + 1 < G:
                        one_hots(n + 1, (n + 1) % 2)
                    add_window(places[n - (G - QUAD)], r * G + n, n % 2)
            dve.wait_ge(win_added, rounds * G + 2)
            V.memset(rr[:], 0.0).then_inc(counted, 1)

            for h in range(NB):
                V.tensor_scalar(link[:, h, :], count[:, h, 0:N], 1.0, None, ALU.min).then_inc(link_set, 1)
            dve.wait_ge(unit_done, upto["xw"])
            dve.wait_ge(link_set, NB)
            for h in range(NB):
                own = slice(h * P, (h + 1) * P)
                dve.wait_ge(link_turned, h + 1)
                V.scalar_tensor_tensor(out=sym[:, h, :], in0=bank[:, h % 2, :].bitcast(BF16), scalar=0.0,
                                       in1=link[:, h, :], op0=ALU.add, op1=ALU.max,
                                       accum_out=degs[:, 0, h:h + 1]).then_inc(sym_max, 1)
                dve.wait_ge(sym_max, h + 1)
                V.tensor_tensor(sym[:, h, own], sym[:, h, own].bitcast(F32), ident[:], ALU.add).then_inc(sym_set, 1)
            V.tensor_scalar(degs[:, 0, :], degs[:, 0, :], 1.0, None, ALU.add).then_inc(deg0_set, 1)
            for h in range(NB):
                own = slice(h * P, (h + 1) * P)
                dve.wait_ge(adj_copied, h + 1)
                V.tensor_tensor(adj[:, h, own], count[:, h, own], ident[:], ALU.add).then_inc(adj_set, 1)

            def low(n, y, of, scale):
                k = n % NB
                dve.wait_ge(hi_set, n + 1)
                V.scalar_tensor_tensor(out=y[1][:, k, :], in0=of, scalar=scale, in1=y[0][:, k, :].bitcast(F32),
                                       op0=ALU.mult, op1=ALU.subtract).then_inc(lo_set, 1)

            def moments(n):
                j = n % NB
                then(V.bn_stats(stats[:], xs[:, j, :]))
                then(V.bn_aggr(mv[:, j, :], stats[:]))
                V.tensor_scalar(veps[:, j:j + 1], mv[:, j, 1:2], EPS, None, ALU.add).then_inc(var_set, 1)

            def residual(n, s, of_bias, scale):
                j, b = n % NB, n % HALF
                dve.wait_ge(hs_done, HALF * s + b + 1)
                dve.wait_ge(biased, of_bias + j + 1)
                V.scalar_tensor_tensor(out=xs[:, j, :], in0=bank[:, HALF * (s % 2) + b, :],
                                       scalar=dinv[:, scale, j:j + 1], in1=xs[:, j, :],
                                       op0=ALU.mult, op1=ALU.add).then_inc(dve_out, 1)
                dve.wait_ge(*freed(s, b))
                moments(n)

            def normalise(n):
                j = n % NB
                dve.wait_ge(rstd_set, n + 1)
                V.tensor_scalar(xs[:, j, :], xs[:, j, :], mv[:, j, 0:1], rstd[:, j:j + 1],
                                ALU.subtract, ALU.mult).then_inc(normed, 1)

            def make_rest(rest, turn):
                for h in range(NB):
                    own = slice(h * P, (h + 1) * P)
                    V.tensor_tensor(rest[:, h, :], count[:, h, 0:N], adj[:, h, :].bitcast(F32),
                                    ALU.subtract).then_inc(rest_part, 1)
                    dve.wait_ge(rest_part, turn * NB + h + 1)
                    ins = V.tensor_tensor(rest[:, h, own], rest[:, h, own].bitcast(F32), ident[:], ALU.add)
                ins.then_inc(rest_set, 1)

            def pairs(b):
                return bank[:, b, 0:2 * NB].rearrange("p (j t) -> p j t", t=2)

            for k in range(NB):
                low(k, ya, xw[:, k, :], dinv[:, 0, k:k + 1])
            dve.wait_ge(deg_summed, 1)
            V.tensor_copy(avec[:, 3, :], pairs(4)[:, :, 0]).then_inc(deg_out, 1)
            dve.wait_ge(deg_out, 1)
            V.tensor_reduce(degmax[:, 0:1], avec[:, 3, :], AX.X, ALU.max).then_inc(degmax_set, 1)
            for j in range(HALF):
                residual(j, 0, 0, 0)
                if j >= 1:
                    normalise(j - 1)
            normalise(HALF - 1)
            dve.wait_ge(degmax_all, 1)
            V.tensor_scalar(flags[0:1, 4:5], degmax[0:1, 1:2], float(EXACT), None, ALU.is_gt).then_inc(big_set, 1)
            dve.wait_ge(big_set, 1)
            big = dve.value_load(flags[0:1, 4:5], min_val=0, max_val=1)
            with dve.If(big > 0):
                dve.wait_ge(hs_done, 2 * HALF)
                make_rest(rest_l1, 0)
                dve.wait_ge(rest_summed, 1)
                V.tensor_tensor(avec[:, 3, :], pairs(0)[:, :, 0], avec[:, 3, :], ALU.add).then_inc(rest_added, 1)
                dve.wait_ge(rest_added, 1)
            V.tensor_copy(degs[:, 1, :], avec[:, 3, :]).then_inc(deg_set, 1)

            def split_vector(v):
                then(V.tensor_copy(ysum[:, :, 0], v))
                V.tensor_tensor(ysum[:, :, 1], v, ysum[:, :, 0].bitcast(F32), ALU.subtract).then_inc(avec_split, 1)

            def take_vector(n):
                dve.wait_ge(avec_summed, n + 1)
                V.tensor_reduce(avec[:, 3, :], pairs(n), AX.X, ALU.add).then_inc(avec_out, 1)
                dve.wait_ge(avec_out, n + 1)
                V.tensor_tensor(avec[:, n, :], avec[:, 3, :], dinv[:, 1, :], ALU.mult)
                then(V.tensor_tensor(avec[:, 2, :], avec[:, 3, :], dinv[:, 2, :], ALU.mult))

            dve.wait_ge(dinv_set, 1)
            split_vector(dinv[:, 1, :])
            for k in range(HALF):
                low(NB + k, yb, xs[:, k, :], dinv[:, 1, k:k + 1])
            for j in range(HALF, NB):
                residual(j, 1, 0, 0)
                if j == HALF:
                    take_vector(0)
                    split_vector(avec[:, 2, :])
                if j == HALF + 2:
                    take_vector(1)
                if j > HALF:
                    normalise(j - 1)
                if j > HALF + 1:
                    low(NB + j - 2, yb, xs[:, j - 2, :], dinv[:, 1, j - 2:j - 1])
            normalise(NB - 1)
            for j in (NB - 2, NB - 1):
                low(NB + j, yb, xs[:, j, :], dinv[:, 1, j:j + 1])

            def add_folds(j):
                dve.wait_ge(biased, NB + j + 1)
                then(V.scalar_tensor_tensor(out=xs[:, j, :], in0=fold1[:], scalar=avec[:, 0, j:j + 1],
                                            in1=xs[:, j, :], op0=ALU.mult, op1=ALU.add))
                then(V.scalar_tensor_tensor(out=xs[:, j, :], in0=fold2[:], scalar=avec[:, 1, j:j + 1],
                                            in1=xs[:, j, :], op0=ALU.mult, op1=ALU.add))

            dve.wait_ge(unit_out, NU)
            for n, y in ((0, ya), (1, yb)):
                for k in range(NB):
                    low((2 + n) * NB + k, y, bank[:, k, :], dinv[:, 2, k:k + 1])
                for j in range(HALF * n, HALF * (n + 1)):
                    add_folds(j)
            for j in range(NB):
                residual(NB + j, 8 + j // HALF, NB, 1)
                if j >= 1:
                    normalise(NB + j - 1)
            normalise(2 * NB - 1)

            V.tensor_reduce(c0[:, FB:FB + 1], c0[:, 0:FB], AX.X, ALU.add)
            for half in range(2):
                s = 11 + 3 * half
                for b in range(HALF):
                    j = HALF * half + b
                    dve.wait_ge(normed, NB + j + 1)
                    then(V.tensor_tensor_reduce(out=fold2[:], in0=xs[:, j, :], in1=urow[:], scale=1.0, scalar=0.0,
                                                op0=ALU.mult, op1=ALU.add, accum_out=rr[:, j:j + 1]))
                    V.tensor_scalar(rr[:, j:j + 1], rr[:, j:j + 1], c0[:, FB:FB + 1], None, ALU.add)
                for b in range(HALF):
                    j = HALF * half + b
                    dve.wait_ge(hs_done, HALF * s + b + 1)
                    V.tensor_tensor(vv[:, j, :], bank[:, HALF * (s % 2) + b, :], biasv[:], ALU.add).then_inc(dve_out, 1)
            dve.wait_ge(dve_out, freed(14, 3)[1])

            def mask_scores(i):
                dve.wait_ge(scored, i + 1)
                dve.wait_ge(masks_set, i + 1)
                if i >= 2:
                    dve.wait_ge(probs_turned, i - 1)
                V.scalar_tensor_tensor(out=score[:, i % 2, :],
                                       in0=bank[:, 2 * (i % 2):2 * (i % 2) + 2, :].rearrange("p a b -> p (a b)"),
                                       scalar=rr[:, i:i + 1], in1=mask[:, i % 2, :],
                                       op0=ALU.add, op1=ALU.mult).then_inc(score_out, 1)
                dve.wait_ge(score_out, i + 1)
                then(V.tensor_tensor_reduce(out=score[:, i % 2, :], in0=score[:, i % 2, :], in1=away[:, i % 2, :],
                                            scale=1.0, scalar=-3.0e38, op0=ALU.add, op1=ALU.max,
                                            accum_out=peak[:, 0, i:i + 1]))
                V.tensor_scalar(peak[:, 1, i:i + 1], peak[:, 0, i:i + 1], -1.0, None, ALU.mult).then_inc(peak_set, 1)

            def attended(i):
                dve.wait_ge(mixed, i + 1)
                dve.wait_ge(probs_set, i + 1)
                then(V.reciprocal(esum[:, 1, i:i + 1], esum[:, 0, i:i + 1]))
                V.scalar_tensor_tensor(out=xs[:, i, :], in0=bank[:, 6 + i % 2, :], scalar=esum[:, 1, i:i + 1],
                                       in1=xs[:, i, :], op0=ALU.mult, op1=ALU.add).then_inc(mixed_out, 1)
                dve.wait_ge(mixed_out, i + 1)
                moments(2 * NB + i)

            for i in range(NB + 1):
                if i < NB:
                    mask_scores(i)
                if i >= 1:
                    attended(i - 1)
                if i >= 2:
                    normalise(2 * NB + i - 2)
            normalise(3 * NB - 1)

            with dve.If(big > 0):
                dve.wait_ge(mixed, NB)
                make_rest(rest_l3, 1)
            for k in range(NB):
                low(4 * NB + k, ya, xs[:, k, :], dinv[:, 1, k:k + 1])

            def hidden_low(k):
                dve.wait_ge(hi_set, 5 * NB + k + 1)
                then(V.tensor_scalar(hidden[:, k % 4, :], hidden[:, k % 4, :], dinv[:, 1, k:k + 1], 0.0,
                                     ALU.mult, ALU.max))
                V.tensor_tensor(ya[1][:, k, :], hidden[:, k % 4, :], ya[0][:, k, :].bitcast(F32),
                                ALU.subtract).then_inc(lo_set, 1)

            for k in range(NB):
                dve.wait_ge(hs_done, 18 * HALF + k + 1)
                V.scalar_tensor_tensor(out=hidden[:, k % 4, :], in0=bank[:, k, :], scalar=dinv[:, 1, k:k + 1],
                                       in1=biasc1[:], op0=ALU.mult, op1=ALU.add).then_inc(dve_out, 1)
                if k >= 1:
                    hidden_low(k - 1)
            hidden_low(NB - 1)
            for j in range(NB):
                residual(3 * NB + j, 22 + j // HALF, 2 * NB, 1)
                if j >= 1:
                    normalise(3 * NB + j - 1)
            normalise(4 * NB - 1)


_INS = ["x", "src", "dst", "L0_gnn_weight", "L0_gnn_bias", "L1_gnn_W1", "L1_gnn_b1", "L1_gnn_W2", "L1_gnn_b2",
        "L1_gnn_W3", "L1_gnn_b3", "L2_gnn_Wq", "L2_gnn_bq", "L2_gnn_Wk", "L2_gnn_bk", "L2_gnn_Wv", "L2_gnn_bv",
        "L3_gnn_W1", "L3_gnn_b1", "L3_gnn_W2", "L3_gnn_b2"]


def kernel(**inputs):
    import numpy as _np
    import concourse.bacc as _bacc
    from concourse import mybir as _mybir
    from concourse.bass_utils import run_bass_kernel_spmd as _run

    nc = _bacc.Bacc("TRN2", target_bir_lowering=False, num_devices=1)
    arrays, args = {}, []
    for name in _INS:
        a = _np.ascontiguousarray(inputs[name])
        arrays[f"in_{name}_dram"] = a
        args.append(nc.dram_tensor(f"in_{name}_dram", a.shape, _mybir.dt.from_np(a.dtype), kind="ExternalInput").ap())
    out = nc.dram_tensor("out_dram", inputs["x"].shape, _mybir.dt.float32, kind="ExternalOutput").ap()
    gnn_kernel(nc, *args, out)
    return _run(nc, [arrays], core_ids=[0]).results[0]["out_dram"]
```

```python
from contextlib import ExitStack

import concourse.bass as bass
from concourse import mybir

ALU = mybir.AluOpType
ACT = mybir.ActivationFunctionType
AX = mybir.AxisListType
F32 = mybir.dt.float32
F32R = mybir.dt.float32r
BF16 = mybir.dt.bfloat16
I32 = mybir.dt.int32
I16 = mybir.dt.int16
U16 = mybir.dt.uint16

P = 128
EPS = 1e-5
NEG = -1000000.0
EXACT = 4096
FAR = 8192.0
CPG = 4
WIN = 40
BY_DVE = 2
EARLY = 24 * 128
SHARE = 1450
BODY = 8
HALF = 4


def gnn_kernel(nc, x, src, dst, w0, b0, w1, b1, w2, b2, w3, b3, wq, bq, wk, bk, wv, bv, v1, c1, v2, c2, out):
    N, D = x.shape
    E = src.shape[0]
    NB = N // P
    FB = D // P
    G = E // (CPG * P)
    GE = CPG * P
    ROUNDS = (N + WIN - 1) // WIN
    KEYS = NB * WIN
    SCALE = float(D) ** -0.5
    assert D == 512 and NB == 2 * HALF and G % BODY == 0 and KEYS <= 512 and G <= P

    with ExitStack() as ctx:
        place = [(nc.sbuf_base + 63) // 64 * 64]

        def region(size):
            start = place[0]
            place[0] += (size + 31) // 32 * 32
            assert place[0] <= nc.sbuf_usable_end
            return start

        def at(name, start, shape, dt):
            return nc.alloc_sbuf_tensor_at(name, shape, dt, offset=start)

        def sb(name, shape, dt):
            size = {F32: 4, F32R: 4, I32: 4, BF16: 2, I16: 2, U16: 2}[dt]
            for n in shape[1:]:
                size *= n
            return at(name, region(size), shape, dt)

        def sem(name):
            return ctx.enter_context(nc.semaphore(name))

        W = D * FB * 4
        adj = sb("adj", [P, NB, N], F32R)
        count = sb("count", [P, NB, N + WIN], U16)
        xs = sb("xs", [P, NB, D], F32)
        r0 = region(2 * W)
        wfold = at("wfold", r0, [P, FB, D], F32)
        mfold = at("mfold", r0 + W, [P, FB, D], F32)
        y3_lo = at("y3_lo", r0, [P, NB, D], F32R)

        r1 = region(4 * W)
        x0t = at("x0t", r1, [P, FB, N], F32)
        w0_sb = at("w0_sb", r1 + 2 * W, [P, FB, D], F32)
        wqt = at("wqt", r1 + 3 * W, [P, FB, D], F32)
        sym = at("sym", r1, [P, NB, N], F32R)
        rest_l1 = at("rest_l1", r1, [P, NB, N], F32R)
        v1_sb = at("v1_sb", r1, [P, FB, D], F32)
        v2_sb = at("v2_sb", r1 + W, [P, FB, D], F32)
        xt = at("xt", r1 + 2 * W, [P, FB, N], F32)
        y3_hi = at("y3_hi", r1 + 2 * W, [P, NB, D], F32R)

        r2 = region(4 * W)
        wq_sb = at("wq_sb", r2, [P, FB, D], F32)
        wk_sb = at("wk_sb", r2 + W, [P, FB, D], F32)
        wkt = at("wkt", r2 + 2 * W, [P, FB, D], F32)
        w2_sb = at("w2_sb", r2 + 3 * W, [P, FB, D], F32)
        w3_sb = at("w3_sb", r2, [P, FB, D], F32)
        w1_sb = at("w1_sb", r2 + W, [P, FB, D], F32)
        w2t = at("w2t", r2 + 2 * W, [P, FB, D], F32)
        w1t = at("w1t", r2 + 2 * W, [P, FB, D], F32)
        w23 = at("w23", r2 + 3 * W, [P, FB, D], F32)
        ya = (at("ya_hi", r2, [P, NB, D], F32R), at("ya_lo", r2 + 2 * W, [P, NB, D], F32R))
        rows_a = at("rows_a", r2 + 2 * W, [P, NB, D], F32)
        gt3 = at("gt3", r2, [P, FB, N], F32)
        score = at("score", r2, [P, 2, N], F32)
        away = at("away", r2 + 2 * N * 4, [P, 2, N], F32)
        probt = at("probt", r2 + 4 * N * 4, [P, 2, NB, P], F32)
        mask = at("mask", r2 + 6 * N * 4, [P, 2, N], BF16)

        r3 = region(4 * W)
        xw = at("xw", r3, [P, NB, D], F32)
        edge_rows = at("edge_rows", r3 + 2 * W, [G, 2, GE], I32)
        bits = at("bits", r3 + 2 * W + 4096, [G, 2, GE], I32)
        key_rows = at("key_rows", r3 + 2 * W + 8192, [G, 3, GE], F32)
        keyed = at("keyed", r3 + 2 * W, [P, 3, CPG * G], F32)
        apart = at("apart", r3 + 2 * W + 8192, [P, 2, CPG - BY_DVE, P], BF16)
        link = at("link", r3 + 2 * W, [P, NB, N], BF16)
        xt1 = at("xt1", r3, [P, FB, N], F32)
        deg_row = at("deg_row", r3 + 2 * W, [1, N], F32)
        yb = (at("yb_hi", r3, [P, NB, D], F32R), at("yb_lo", r3 + 2 * W, [P, NB, D], F32R))
        rows_b = at("rows_b", r3 + 2 * W, [P, NB, D], F32)
        vv = at("vv", r3, [P, NB, D], F32)
        tt = at("tt", r3 + 2 * W, [P, FB, N], F32)
        rest_l3 = at("rest_l3", r3, [P, NB, N], F32R)

        r4 = region(W)
        hot_lo = at("hot_lo", r4, [P, 2 * CPG, P], BF16)
        hot_key = at("hot_key", r4 + 2 * CPG * P * 2, [P, 2 * CPG, KEYS], BF16)
        wv_sb = at("wv_sb", r4, [P, FB, D], F32)
        hidden = at("hidden", r4, [P, 4, D], F32)

        edge_key = sb("edge_key", [P, 3, CPG * G], F32)
        bias0 = sb("bias0", [P, D], F32)
        bias3 = sb("bias3", [P, D], F32)
        biasv = sb("biasv", [P, D], F32)
        biasc1 = sb("biasc1", [P, D], F32)
        biasc2 = bias0
        fold1 = sb("fold1", [P, D], F32)
        fold2 = sb("fold2", [P, D], F32)
        urow = sb("urow", [P, D], F32)

        ident = sb("ident", [P, P], F32)
        identb = sb("identb", [P, P], BF16)
        ones = sb("ones", [P, P], F32)
        ones2 = sb("ones2", [P, 2], F32R)
        col_lo = sb("col_lo", [P, P], I16)
        col_key = sb("col_key", [P, KEYS], I16)
        span_at = sb("span_at", [P, ROUNDS], F32)
        bcol = sb("bcol", [P, 4, FB], F32)
        brow = sb("brow", [4 * FB, P], F32)
        bqb = sb("bqb", [P, FB], F32)
        group_lim = sb("group_lim", [G, 4], F32)
        group_dia = sb("group_dia", [G, 2, G], F32)
        group_row = sb("group_row", [P, 2, G], F32)
        base_at = sb("base_at", [1, G], I32)
        rounds_f = sb("rounds_f", [P, ROUNDS + 2], F32)
        flags = sb("flags", [1, 8], I32)
        shift = sb("shift", [P, 1], F32)
        tb = sb("tb", [P, FB], F32)
        c0 = sb("c0", [P, FB + 1], F32)
        degs = sb("degs", [P, 2, NB], F32)
        degmax = sb("degmax", [P, 2], F32)
        dinv = sb("dinv", [P, 2, NB], F32)
        mhalf = sb("mhalf", [P, NB], F32)
        stats = sb("stats", [P, 6], F32)
        mv = sb("mv", [P, NB, 2], F32)
        veps = sb("veps", [P, NB], F32)
        rstd = sb("rstd", [P, NB], F32)
        rr = sb("rr", [P, NB], F32)
        peak = sb("peak", [P, 2, NB], F32)
        esum = sb("esum", [P, 2, NB], F32)

        bank = ctx.enter_context(nc.psum_tensor("bank", [P, 8, 512], F32))

        edges_in = sem("edges_in")
        x_in = [sem("x_in_low"), sem("x_in_high")]
        w_in = {k: sem("w_in_" + k) for k in ("q", "k", "0", "2", "3", "1", "v", "v1", "v2")}
        cols_in, rows_in = sem("cols_in"), sem("rows_in")
        const_set = sem("const_set")
        dve_set = sem("dve_set")
        pool_set = sem("pool_set")
        rows_set = sem("rows_set")
        rows_turned = sem("rows_turned")
        rounds_set = sem("rounds_set")
        round_set = sem("round_set")
        hot_set = sem("hot_set")
        apart_set = sem("apart_set")
        act_hot_set = sem("act_hot_set")
        win_summed = sem("win_summed")
        win_added = sem("win_added")
        counted = sem("counted")
        bqb_set = sem("bqb_set")
        unit_done = sem("unit_done")
        unit_out = sem("unit_out")
        link_set = sem("link_set")
        link_turned = sem("link_turned")
        sym_max = sem("sym_max")
        sym_set = sem("sym_set")
        adj_copied = sem("adj_copied")
        adj_set = sem("adj_set")
        dinv0_set = sem("dinv0_set")
        row_summed, row_out = sem("row_summed"), sem("row_out")
        deg_summed, deg_out = sem("deg_summed"), sem("deg_out")
        degmax_set, degmax_all = sem("degmax_set"), sem("degmax_all")
        big_set = sem("big_set")
        rest_set = sem("rest_set")
        rest_part = sem("rest_part")
        deg_set, dinv_set = sem("deg_set"), sem("dinv_set")
        hi_set, lo_set = sem("hi_set"), sem("lo_set")
        hs_done = sem("hs_done")
        act_out, dve_out = sem("act_out"), sem("dve_out")
        var_set, rstd_set = sem("var_set"), sem("rstd_set")
        normed = sem("normed")
        biased = sem("biased")
        masks_set = sem("masks_set")
        scored = sem("scored")
        score_out = sem("score_out")
        peak_set = sem("peak_set")
        probs_set = sem("probs_set")
        probs_turned = sem("probs_turned")
        probt_set = sem("probt_set")
        mixed = sem("mixed")
        mixed_out = sem("mixed_out")
        stored = sem("stored")

        def each(kind, h=0):
            return [(kind, f, h) for f in range(FB)]

        def xw_units(first, last):
            return [("xw", j, 0) for j in range(first, last)]

        UNITS = each("xT", 0) + xw_units(0, 3) + each("xT", 1) + xw_units(3, NB - 2)
        UNITS += each("wqT") + each("wkT") + [("bT", 0, 0)] + xw_units(NB - 2, NB - 1)
        UNITS += each("m") + [("tb", 0, 0), ("u", 0, 0)] + each("w2T") + xw_units(NB - 1, NB)
        UNITS += each("w23") + each("w1T") + [("g1", 0, 0)] + each("wf") + [("g2", 0, 0)]
        NU = len(UNITS)
        upto = {kind: n + 1 for n, (kind, _, _) in enumerate(UNITS)}

        def unit_bank(n):
            return bank[:, HALF + (n % 4 if n < NU - 1 else 3), :]

        def weight_of(m):
            kind = UNITS[m // 4][0]
            return {"T": P, "b": D // 2}.get(kind[-1], FB * P * 2)

        pieces = {}
        n, credit = 0, EARLY
        for g in range(-1, G):
            m = n
            while credit > 0 and m < 4 * (NU - 1):
                credit -= weight_of(m)
                m += 1
            pieces[g] = (n, m)
            n = m
            credit = min(credit, 0) + SHARE
        ALONG = n
        UA = n // 4

        EAGER = NB - 4
        y3 = (y3_hi, y3_lo)

        WHO = "DD" "AL" "AL" "DD" "DD" "DD" "ADA" "ADA" "AA" "DD" "AA" "DD"
        def freed(s, b):
            who = WHO[s]
            n = HALF * WHO[:s].count(who) + b + 1
            if who == "L":
                return lo_set, NB + n
            return (act_out if who == "A" else dve_out), n

        block = ctx.enter_context(nc.Block())

        def turned_at(i):
            return 0 if i == NB - 2 else HALF

        def wview(w):
            return w.rearrange("(c p) n -> p c n", p=P)

        @block.sync
        def _(sp):
            sp.dma_start(edge_rows[:, 0, :], dst.rearrange("(g e) -> g e", e=GE)).then_inc(edges_in, 16)
            sp.dma_start(edge_rows[:, 1, :], src.rearrange("(g e) -> g e", e=GE)).then_inc(edges_in, 16)
            for h in range(2):
                sp.dma_start(xs[:, HALF * h:HALF * (h + 1), :],
                             x[h * D:(h + 1) * D, :].rearrange("(b p) d -> p b d", p=P)).then_inc(x_in[h], 16)
                if h == 0:
                    sp.dma_start(w0_sb[:], wview(w0)).then_inc(w_in["0"], 16)
            sp.dma_start(wq_sb[:], wview(wq)).then_inc(w_in["q"], 16)
            sp.dma_start(wk_sb[:], wview(wk)).then_inc(w_in["k"], 16)
            for n, b in enumerate((bq, bk, b1, b2)):
                sp.dma_start(brow[n * FB:(n + 1) * FB, :], b.rearrange("(c p) -> c p", p=P)).then_inc(cols_in, 16)
            for t, b in ((bias0, b0), (bias3, b3), (biasv, bv), (biasc1, c1)):
                sp.dma_start(t[:], b.partition_broadcast(P)).then_inc(rows_in, 16)
            sp.dma_start(w2_sb[:], wview(w2)).then_inc(w_in["2"], 16)
            sp.wait_ge(unit_done, upto["u"])
            sp.dma_start(w3_sb[:], wview(w3)).then_inc(w_in["3"], 16)
            sp.dma_start(w1_sb[:], wview(w1)).then_inc(w_in["1"], 16)
            sp.wait_ge(counted, 1)
            sp.dma_start(wv_sb[:], wview(wv)).then_inc(w_in["v"], 16)
            sp.wait_ge(hs_done, HALF * 12)
            sp.dma_start(v1_sb[:], wview(v1)).then_inc(w_in["v1"], 16)
            sp.dma_start(v2_sb[:], wview(v2)).then_inc(w_in["v2"], 16)
            sp.dma_start(biasc2[:], c2.partition_broadcast(P)).then_inc(rows_in, 16)
            for j in range(NB):
                sp.wait_ge(normed, 3 * NB + j + 1)
                sp.dma_start(out[j * P:(j + 1) * P, :], xs[:, j, :]).then_inc(stored, 16)
            sp.wait_ge(stored, 16 * NB)

        @block.gpsimd
        def _(pool):
            chain = [0]

            def then(ins):
                chain[0] += 1
                ins.then_inc(pool_set, 1)
                pool.wait_ge(pool_set, chain[0])

            then(nc.gpsimd.memset(ident[:], 0.0))
            then(nc.gpsimd.affine_select(out=ident[:], in_=ident[:], compare_op=ALU.not_equal, fill=1.0,
                                         base=0, pattern=[[-1, P]], channel_multiplier=1))
            nc.gpsimd.tensor_copy(identb[:], ident[:])
            nc.gpsimd.iota(span_at[:], pattern=[[WIN, ROUNDS]], base=0, channel_multiplier=0,
                           allow_small_or_imprecise_dtypes=True)
            nc.gpsimd.memset(ones[:], 1.0).then_inc(const_set, 1)
            nc.gpsimd.iota(col_lo[:], pattern=[[1, P]], base=0, channel_multiplier=0,
                           allow_small_or_imprecise_dtypes=True)
            nc.gpsimd.iota(col_key[:], pattern=[[1, KEYS]], base=0, channel_multiplier=0,
                           allow_small_or_imprecise_dtypes=True)
            nc.gpsimd.memset(mhalf[:], -0.5)
            nc.gpsimd.memset(ones2[:].bitcast(F32), 1.0).then_inc(const_set, 1)
            nc.gpsimd.memset(count[:].bitcast(F32), 0.0).then_inc(const_set, 1)
            pool.wait_ge(unit_out, upto["bT"])
            nc.gpsimd.tensor_tensor(bqb[:], bcol[:, 0, :], bcol[:, 1, :], ALU.mult).then_inc(bqb_set, 1)
            pool.wait_ge(rows_in, 16 * 4)
            pool.wait_ge(unit_done, upto["xT"])
            for j in range(NB):
                nc.gpsimd.tensor_tensor(xs[:, j, :], xs[:, j, :], bias0[:], ALU.add).then_inc(biased, 1)
            for h in range(NB):
                own = slice(h * P, (h + 1) * P)
                pool.wait_ge(sym_max, h + 1)
                then(nc.gpsimd.tensor_scalar(degs[:, 0, h:h + 1], degs[:, 0, h:h + 1], 1.0, None, ALU.add))
                nc.gpsimd.tensor_tensor(dinv[:, 0, h:h + 1], degs[:, 0, h:h + 1], mhalf[:, h:h + 1],
                                        ALU.pow).then_inc(dinv0_set, 1)
                nc.gpsimd.tensor_tensor(sym[:, h, own], sym[:, h, own].bitcast(F32), ident[:],
                                        ALU.add).then_inc(sym_set, 1)
                pool.wait_ge(adj_copied, h + 1)
                nc.gpsimd.tensor_tensor(adj[:, h, own], adj[:, h, own].bitcast(F32), ident[:],
                                        ALU.add).then_inc(adj_set, 1)
            def inverse_roots(first, last):
                for n in range(first, last):
                    j = n % NB
                    pool.wait_ge(var_set, n + 1)
                    nc.gpsimd.tensor_tensor(rstd[:, j:j + 1], veps[:, j:j + 1], mhalf[:, j:j + 1],
                                            ALU.pow).then_inc(rstd_set, 1)

            inverse_roots(0, 1)
            pool.wait_ge(degmax_set, 1)
            nc.gpsimd.partition_all_reduce(degmax[:, 1:2], degmax[:, 0:1], P,
                                           bass.bass_isa.ReduceOp.max).then_inc(degmax_all, 1)
            inverse_roots(1, HALF)
            pool.wait_ge(deg_set, 1)
            nc.gpsimd.tensor_tensor(dinv[:, 1, :], degs[:, 1, :], mhalf[:], ALU.pow).then_inc(dinv_set, 1)
            inverse_roots(HALF, NB)
            for j in range(NB):
                pool.wait_ge(hs_done, HALF * (3 if j < HALF else 5))
                nc.gpsimd.tensor_tensor(xs[:, j, :], xs[:, j, :], bias3[:], ALU.add).then_inc(biased, 1)
            inverse_roots(NB, 2 * NB)
            pool.wait_ge(*freed(12, 0))
            for i in range(NB):
                if i >= 2:
                    pool.wait_ge(peak_set, i - 1)
                then(nc.gpsimd.tensor_scalar(mask[:, i % 2, :], count[:, i, 0:N], 1.0, None, ALU.min))
                nc.gpsimd.tensor_scalar(away[:, i % 2, :], mask[:, i % 2, :], -1.0, -NEG,
                                        ALU.add, ALU.mult).then_inc(masks_set, 1)
                if i >= 2:
                    inverse_roots(2 * NB + i - 2, 2 * NB + i - 1)
            inverse_roots(3 * NB - 2, 3 * NB)
            pool.wait_ge(rows_in, 16 * 5)
            for j in range(NB):
                pool.wait_ge(lo_set, 4 * NB + j + 1)
                nc.gpsimd.tensor_tensor(xs[:, j, :], xs[:, j, :], biasc2[:], ALU.add).then_inc(biased, 1)
            inverse_roots(3 * NB, 4 * NB)

        @block.tensor
        def _(pe):
            def piece(m):
                n, k = m // 4, m % 4
                kind, f, h = UNITS[n]
                to = unit_bank(n)
                if k == 0 and n >= 4:
                    pe.wait_ge(unit_out, n - 3 if n < NU - 1 else n)
                first, last = k == 0, k == FB - 1
                cols = slice(k * P, (k + 1) * P)
                rows = slice(f * P, (f + 1) * P)
                if kind == "xT":
                    pe.wait_ge(x_in[h], 16)
                    mm = pe.transpose(to[:, cols], xs[:, 4 * h + k, rows], ident[:])
                elif kind in ("wqT", "wkT", "w2T", "w1T"):
                    w = {"wqT": wq_sb, "wkT": wk_sb, "w2T": w2_sb, "w1T": w1_sb}[kind]
                    pe.wait_ge(w_in[kind[1]], 16)
                    mm = pe.transpose(to[:, cols], w[:, k, rows], ident[:])
                elif kind == "bT":
                    if not last:
                        return
                    pe.wait_ge(cols_in, 16 * 4)
                    mm = pe.transpose(to[:, 0:4 * FB], brow[:], ident[0:4 * FB, 0:4 * FB])
                elif kind == "m":
                    pe.wait_ge(unit_out, upto["wkT"])
                    mm = pe.matmul(to, wqt[:, k, rows], wkt[:, k, :], start=first, stop=last)
                elif kind == "tb":
                    pe.wait_ge(unit_out, upto["bT"])
                    for c in range(FB):
                        mm = pe.matmul(to[:, k:k + 1], wkt[:, c, cols], bcol[:, 0, c:c + 1],
                                       start=c == 0, stop=c == FB - 1)
                    if last:
                        pe.wait_ge(bqb_set, 1)
                        mm = pe.matmul(to[:, FB:2 * FB], ones[:], bqb[:], start=True, stop=True)
                elif kind in ("u", "g1", "g2"):
                    pe.wait_ge(unit_out, upto["bT"])
                    n_b, w = {"u": (1, wqt), "g1": (3, w3_sb), "g2": (2, w23)}[kind]
                    if kind == "g1":
                        pe.wait_ge(w_in["3"], 16)
                    if kind == "g2":
                        pe.wait_ge(unit_out, upto["w23"])
                    mm = pe.matmul(to, bcol[:, n_b, k:k + 1].to_broadcast([P, P]), w[:, k, :],
                                   start=first, stop=last)
                elif kind == "xw":
                    pe.wait_ge(w_in["0"], 16)
                    pe.wait_ge(unit_out, FB if f < HALF else upto["xT"])
                    mm = pe.matmul(to, x0t[:, k, rows], w0_sb[:, k, :], start=first, stop=last)
                elif kind == "w23":
                    pe.wait_ge(w_in["3"], 16)
                    pe.wait_ge(unit_out, upto["w2T"])
                    mm = pe.matmul(to, w2t[:, k, rows], w3_sb[:, k, :], start=first, stop=last)
                elif kind == "wf":
                    pe.wait_ge(unit_out, upto["w1T"])
                    mm = pe.matmul(to, w1t[:, k, rows], w23[:, k, :], start=first, stop=last)
                if last:
                    mm.then_inc(unit_done, 1)

            pe.wait_ge(const_set, 1)
            pe.wait_ge(rows_set, 1)
            pe.matmul(bank[:, 0, 0:2 * G], ones[0:G, :], group_dia[:].rearrange("g a b -> g (a b)"),
                      start=True, stop=True).then_inc(rows_turned, 1)
            pe.wait_ge(rows_set, 2)
            for n in range(3):
                for c in range(CPG):
                    at_col = ((n % 2) * CPG + c) * G
                    mm = pe.transpose(bank[:, 2 + n // 2, at_col:at_col + G],
                                      key_rows[:, n, c * P:(c + 1) * P], ident[0:G, 0:G])
            mm.then_inc(rows_turned, 1)

            def chunk(at_hot, at_bank, c):
                return pe.matmul(bank[:, at_bank, 0:KEYS], hot_lo[:, at_hot, :], hot_key[:, at_hot, :],
                                 start=c == 0, stop=c == CPG - 1)

            for m in range(*pieces[-1]):
                piece(m)
            for g in range(G):
                pe.wait_ge(win_added, g + 1)
                for c in range(CPG):
                    pe.wait_ge(hot_set, CPG * g + c + 1)
                    if c == BY_DVE:
                        pe.wait_ge(act_hot_set, g + 1)
                    mm = chunk((g % 2) * CPG + c, g % 2, c)
                mm.then_inc(win_summed, 1)
                for m in range(*pieces[g]):
                    piece(m)
            pe.wait_ge(rounds_set, 1)
            rounds = pe.value_load(flags[0:1, 0:1], min_val=1, max_val=ROUNDS)
            with pe.If(rounds > 1):
                with pe.Fori(1, rounds) as r:
                    with pe.Fori(0, G // BODY) as q:
                        for n in range(BODY):
                            pe.wait_ge(win_added, r * G + q * BODY + (n + 1))
                            for c in range(CPG):
                                pe.wait_ge(hot_set, (r * G + q * BODY) * CPG + (n * CPG + c + 1))
                                if c == BY_DVE:
                                    pe.wait_ge(act_hot_set, r * G + q * BODY + (n + 1))
                                mm = chunk((n % 2) * CPG + c, n % 2, c)
                            mm.then_inc(win_summed, 1)
                pe.nop()

            def turn_links(h):
                if h == 0:
                    pe.wait_ge(unit_out, NU - 1)
                if h >= 3:
                    pe.wait_ge(sym_max, h - 2)
                to = bank[:, HALF + h % 3, :].bitcast(BF16)
                for j in range(NB):
                    if h == 0:
                        pe.wait_ge(link_set, j + 1)
                    mm = pe.transpose(to[:, j * P:(j + 1) * P], link[:, j, h * P:(h + 1) * P], identb[:])
                mm.then_inc(link_turned, 1)

            for m in range(ALONG, 4 * (NU - 1)):
                piece(m)

            def rows_step(s, mat, y, lo_from, more=None, before={}):
                for k in range(NB):
                    if k in before:
                        before[k]()
                    pe.wait_ge(lo_set, lo_from + k + 1)
                    if s < 2:
                        pe.wait_ge(sym_set, k + 1)
                    for b in range(HALF):
                        j = HALF * (s % 2) + b
                        if k == 0:
                            bank_free(s, b)
                        to = bank[:, HALF * (s % 2) + b, :]
                        for m in [mat] + ([more] if more is not None else []):
                            for part in range(2):
                                mm = pe.matmul(to, m[:, k, j * P:(j + 1) * P], y[part][:, k, :],
                                               start=k == 0 and part == 0 and m is mat,
                                               stop=k == NB - 1 and part == 1 and (more is None or m is more))
                        if k == NB - 1:
                            mm.then_inc(hs_done, 1)

            def cols_step(s, mat, y, lo_from, more=None):
                half = slice((s % 2) * D, (s % 2 + 1) * D)
                for k in range(NB):
                    pe.wait_ge(lo_set, lo_from + k + 1)
                    for f in range(FB):
                        if k == 0:
                            bank_free(s, f)
                        to = bank[:, HALF * (s % 2) + f, :]
                        for m in [mat] + ([more] if more is not None else []):
                            for part in range(2):
                                mm = pe.matmul(to, y[part][:, k, f * P:(f + 1) * P], m[:, k, half],
                                               start=k == 0 and part == 0 and m is mat,
                                               stop=k == NB - 1 and part == 1 and (more is None or m is more))
                        if k == NB - 1:
                            mm.then_inc(hs_done, 1)

            def bank_free(s, b):
                if s == 0:
                    if b == 0:
                        pe.wait_ge(counted, 1)
                elif s == 1:
                    if b == 2:
                        pe.wait_ge(row_out, 1)
                elif s == 18:
                    if b == 0:
                        pe.wait_ge(score_out, NB)
                        pe.wait_ge(probt_set, NB - 1)
                elif s == 19:
                    if b == 0:
                        pe.wait_ge(probt_set, NB)
                        pe.wait_ge(mixed_out, NB)
                else:
                    if s == 2 and b == 0:
                        pe.wait_ge(row_out, 1)
                        pe.wait_ge(deg_out, 1)
                    pe.wait_ge(*freed(s - 2, b))

            def weight_step(s, half, g, w, g_from):
                for b in range(HALF):
                    bank_free(s, b)
                    j = HALF * half + b
                    for k in range(FB):
                        if b == 0:
                            pe.wait_ge(*freed(g_from, k))
                        mm = pe.matmul(bank[:, HALF * (s % 2) + b, :], g[:, k, j * P:(j + 1) * P], w[:, k, :],
                                       start=k == 0, stop=k == FB - 1)
                    mm.then_inc(hs_done, 1)

            def degree_row(mat, first):
                for half in range(2):
                    for k in range(NB):
                        mm = pe.matmul(bank[0:2, first + half, :], ones2[:], mat[:, k, half * D:(half + 1) * D],
                                       start=k == 0, stop=k == NB - 1)
                mm.then_inc(row_summed, 1)

            def degree_cols(turn, to):
                pe.wait_ge(row_out, turn + 1)
                for j in range(NB):
                    mm = pe.matmul(bank[:, to, j:j + 1], deg_row[0:1, j * P:(j + 1) * P], ones[0:1, 0:1],
                                   start=True, stop=True)
                mm.then_inc(deg_summed, 1)

            def turn_step(s, half, norms):
                for f in range(FB):
                    bank_free(s, f)
                    for b in range(HALF):
                        j = HALF * half + b
                        pe.wait_ge(normed, norms + j + 1)
                        mm = pe.transpose(bank[:, HALF * (s % 2) + f, b * P:(b + 1) * P],
                                          xs[:, j, f * P:(f + 1) * P], ident[:])
                    mm.then_inc(hs_done, 1)

            def turn_first():
                for h in range(3):
                    turn_links(h)
                for m in range(4 * (NU - 1), 4 * NU):
                    piece(m)

            turns = {0: turn_first}
            for k in range(1, NB - 2):
                turns[k] = lambda h=k + 2: turn_links(h)

            def degrees():
                pe.wait_ge(adj_set, NB)
                pe.wait_ge(const_set, 2)
                pe.wait_ge(sym_max, NB - 2)
                pe.wait_ge(unit_out, NU)
                degree_row(adj, HALF + 2)

            turns[NB - 1] = degrees
            rows_step(0, sym, ya, 0, before=turns)

            def first_degrees():
                pe.wait_ge(*freed(0, 0))
                degree_cols(0, 0)

            def load_big():
                pe.wait_ge(big_set, 1)
                big_at_pe.append(pe.value_load(flags[0:1, 4:5], min_val=0, max_val=1))

            big_at_pe = []
            rows_step(1, sym, ya, 0, before={2: first_degrees, NB - 1: load_big})
            big = big_at_pe[0]
            with pe.If(big > 0):
                pe.wait_ge(rest_set, 1)
                pe.wait_ge(*freed(0, 2))
                degree_row(rest_l1, 1)
                degree_cols(1, 3)
                pe.wait_ge(deg_out, 2)
                pe.nop()

            for half in range(2):
                turn_step(2 + 2 * half, half, 0)
                weight_step(3 + 2 * half, half, xt1, wfold, 2 + 2 * half)

            def layer1(mats):
                more = mats[1] if len(mats) > 1 else None
                for s, y, lo_from in ((6, ya, NB), (8, yb, 2 * NB), (10, ya, 3 * NB)):
                    for half in range(2):
                        rows_step(s + half, adj, y, lo_from, more)

            with pe.If(big > 0):
                layer1([adj, rest_l1])
            with pe.Else():
                layer1([adj])

            pe.wait_ge(w_in["v"], 16)
            for half in range(2):
                s = 12 + 3 * half
                turn_step(s, half, NB)
                weight_step(s + 1, half, xt, wv_sb, s)
                for f in range(FB):
                    bank_free(s + 2, f)
                    for k in range(FB):
                        mm = pe.matmul(bank[:, HALF * (s % 2) + f, :], mfold[:, k, f * P:(f + 1) * P],
                                       xt[:, k, half * D:(half + 1) * D], start=k == 0, stop=k == FB - 1)
                    mm.then_inc(hs_done, 1)

            def scores(i):
                pe.wait_ge(*freed(14 if i < HALF else 17, 3))
                if i >= 2:
                    pe.wait_ge(score_out, i - 1)
                for c in range(2):
                    if i < 2:
                        pe.wait_ge(*freed(16, 2 * i + c))
                    for k in range(FB):
                        mm = pe.matmul(bank[:, 2 * (i % 2) + c, :], tt[:, k, i * P:(i + 1) * P],
                                       xt[:, k, c * D:(c + 1) * D], start=k == 0, stop=k == FB - 1)
                mm.then_inc(scored, 1)

            def turn_probs(i):
                pe.wait_ge(probs_set, i + 1)
                pe.wait_ge(*(freed(17, 1) if i == 0 else (score_out, i + 1) if i == NB - 2
                             else (probt_set, min(i, NB - 2))))
                for j in range(NB):
                    mm = pe.transpose(bank[:, turned_at(i) + j // 4, (j % 4) * P:(j % 4 + 1) * P],
                                      score[:, i % 2, j * P:(j + 1) * P], ident[:])
                mm.then_inc(probs_turned, 1)

            def mix(i):
                pe.wait_ge(probt_set, i + 1)
                pe.wait_ge(*(freed(17, 2 + i) if i < 2 else (mixed_out, i - 1)))
                if i == 0:
                    pe.wait_ge(*freed(16, 3))
                for j in range(NB):
                    mm = pe.matmul(bank[:, 6 + i % 2, :], probt[:, i % 2, j, :], vv[:, j, :],
                                   start=j == 0, stop=j == NB - 1)
                mm.then_inc(mixed, 1)

            pe.wait_ge(*freed(15, 3))
            scores(0)
            scores(1)
            for i in range(NB - 2):
                turn_probs(i)
                scores(i + 2)
                if i == NB - 3:
                    turn_probs(NB - 2)
                mix(i)
            turn_probs(NB - 1)
            mix(NB - 2)
            mix(NB - 1)

            def layer3(mats):
                more = mats[1] if len(mats) > 1 else None
                for n, w in enumerate((v1_sb, v2_sb)):
                    for half in range(2):
                        cols_step(18 + 4 * n + half, adj, y3, (4 + n) * NB, more)
                    pe.wait_ge(w_in["v1" if n == 0 else "v2"], 16)
                    for half in range(2):
                        weight_step(20 + 4 * n + half, half, gt3, w, 18 + 4 * n + half)

            with pe.If(big > 0):
                pe.wait_ge(rest_set, 2)
                layer3([adj, rest_l3])
            with pe.Else():
                layer3([adj])

        @block.scalar
        def _(act):
            def copy_unit(n):
                kind, f, h = UNITS[n]
                at_bank = unit_bank(n)
                act.wait_ge(unit_done, n + 1)
                if kind == "w2T" and f == 0:
                    act.wait_ge(unit_done, upto["u"])
                if kind == "xT":
                    ins = nc.scalar.copy(x0t[:, f, h * D:(h + 1) * D], at_bank)
                elif kind == "bT":
                    ins = nc.scalar.copy(bcol[:].rearrange("p n c -> p (n c)"), at_bank[:, 0:4 * FB])
                elif kind == "m":
                    ins = nc.scalar.mul(mfold[:, f, :], at_bank, SCALE)
                elif kind == "tb":
                    nc.scalar.mul(tb[:], at_bank[:, 0:FB], SCALE)
                    ins = nc.scalar.mul(c0[:, 0:FB], at_bank[:, FB:2 * FB], SCALE)
                elif kind == "u":
                    ins = nc.scalar.mul(urow[:], at_bank, SCALE)
                else:
                    to = {"wqT": wqt, "wkT": wkt, "xw": xw, "w2T": w2t, "w23": w23, "w1T": w1t,
                          "wf": wfold, "g1": fold1, "g2": fold2}[kind]
                    ins = nc.scalar.copy(to[:, f, :] if kind[0] != "g" else to[:], at_bank)
                ins.then_inc(unit_out, 1)

            def low_one_hots(g, slot, before):
                for c in range(BY_DVE, CPG):
                    ins = nc.scalar.activation(apart[:, slot, c - BY_DVE, :], col_lo[:], ACT.Abs, scale=-1.0,
                                               bias=edge_key[:, 0, bass.ds(g + c * G, 1)])
                ins.then_inc(apart_set, 1)
                act.wait_ge(apart_set, before + 1)
                nc.scalar.activation(hot_lo[:, slot * CPG + BY_DVE:(slot + 1) * CPG, :], apart[:, slot], ACT.Relu,
                                     scale=-1.0, bias=ones[:, 0:1]).then_inc(act_hot_set, 1)

            act.wait_ge(const_set, 2)
            for n in range(pieces[-1][1] // 4):
                copy_unit(n)
            act.wait_ge(win_added, 1)
            for g in range(G):
                if g >= 2:
                    act.wait_ge(win_summed, g - 1)
                low_one_hots(g, g % 2, g)
                if g >= 2:
                    for n in range(pieces[g - 2][0] // 4, pieces[g - 2][1] // 4):
                        copy_unit(n)
            for n in range(pieces[G - 2][0] // 4, UA):
                copy_unit(n)
            act.wait_ge(rounds_set, 1)
            rounds = act.value_load(flags[0:1, 0:1], min_val=1, max_val=ROUNDS)
            with act.If(rounds > 1):
                with act.Fori(1, rounds) as r:
                    with act.Fori(0, G // BODY) as q:
                        for n in range(BODY):
                            act.wait_ge(win_summed, r * G + q * BODY + (n - 1))
                            low_one_hots(q * BODY + n, n % 2, r * G + q * BODY + n)
                act.nop()
            for n in range(UA, NU - 1):
                copy_unit(n)

            act.wait_ge(counted, 1)
            act.wait_ge(unit_out, NU - 1)
            for k in range(NB):
                nc.scalar.copy(adj[:, k, :], count[:, k, 0:N]).then_inc(adj_copied, 1)
                act.wait_ge(dinv0_set, k + 1)
                nc.scalar.activation(ya[0][:, k, :], xw[:, k, :], ACT.Copy, scale=dinv[:, 0, k:k + 1]).then_inc(hi_set, 1)
                if k == 0:
                    copy_unit(NU - 1)
            def copy_cols(s, half, to, bias=None):
                for f in range(FB):
                    act.wait_ge(hs_done, s * HALF + f + 1)
                    at_bank = bank[:, HALF * (s % 2) + f, :]
                    to_f = to[:, f, half * D:(half + 1) * D]
                    if bias is None:
                        nc.scalar.copy(to_f, at_bank).then_inc(act_out, 1)
                    else:
                        nc.scalar.activation(to_f, at_bank, ACT.Identity, bias=bias[:, f:f + 1]).then_inc(act_out, 1)

            def high(y, k, of):
                nc.scalar.activation(y[0][:, k, :], of, ACT.Copy, scale=dinv[:, 1, k:k + 1]).then_inc(hi_set, 1)

            act.wait_ge(dinv_set, 1)
            for half in range(2):
                copy_cols(2 + 2 * half, half, xt1)
                for b in range(HALF):
                    act.wait_ge(hs_done, (3 + 2 * half) * HALF + b + 1)
                    high(ya, half * HALF + b, bank[:, HALF + b, :])
            for s, y, rows in ((6, yb, rows_b), (8, ya, rows_a)):
                for k in range(NB):
                    act.wait_ge(*freed(s + k // HALF, k % HALF))
                    high(y, k, rows[:, k, :])
            for half in range(2):
                copy_cols(12 + 3 * half, half, xt)
                copy_cols(14 + 3 * half, half, tt, tb)
            for i in range(NB):
                act.wait_ge(peak_set, i + 1)
                nc.scalar.activation(score[:, i % 2, :], score[:, i % 2, :], ACT.Exp, bias=peak[:, 1, i:i + 1],
                                     accum_out=esum[:, 0, i:i + 1]).then_inc(probs_set, 1)
                if i == NB - 1:
                    for k in range(EAGER):
                        act.wait_ge(normed, 2 * NB + k + 1)
                        high(y3, k, xs[:, k, :])
                act.wait_ge(probs_turned, i + 1)
                if i >= 2:
                    act.wait_ge(mixed, i - 1)
                nc.scalar.copy(probt[:, i % 2, :, :].rearrange("p j q -> p (j q)"),
                               bank[:, turned_at(i):turned_at(i) + 2, :].rearrange("p a b -> p (a b)")).then_inc(probt_set, 1)
            for k in range(EAGER, NB):
                act.wait_ge(normed, 2 * NB + k + 1)
                high(y3, k, xs[:, k, :])
            copy_cols(18, 0, gt3)
            copy_cols(19, 1, gt3)
            for k in range(NB):
                act.wait_ge(*freed(20 + k // HALF, k % HALF))
                nc.scalar.activation(y3[0][:, k, :], hidden[:, k % 4, :], ACT.Relu,
                                     scale=dinv[:, 1, k:k + 1]).then_inc(hi_set, 1)
            copy_cols(22, 0, gt3)
            copy_cols(23, 1, gt3)

        @block.vector
        def _(dve):
            V = nc.vector
            chain = [0]

            def then(ins):
                chain[0] += 1
                ins.then_inc(dve_set, 1)
                dve.wait_ge(dve_set, chain[0])

            dve.wait_ge(edges_in, 32)
            V.tensor_reduce(group_lim[:, 0:1], edge_rows[:, 0, :], AX.X, ALU.min)
            then(V.tensor_reduce(group_lim[:, 1:2], edge_rows[:, 0, :], AX.X, ALU.max))
            then(V.tensor_tensor(group_lim[:, 2:3], group_lim[:, 1:2], group_lim[:, 0:1], ALU.subtract))
            dve.wait_ge(const_set, 1)
            V.tensor_scalar(group_dia[:, 0, :], ident[0:G, 0:G], group_lim[:, 0:1], None, ALU.mult)
            V.tensor_scalar(group_dia[:, 1, :], ident[0:G, 0:G], group_lim[:, 2:3], None,
                            ALU.mult).then_inc(rows_set, 1)
            V.tensor_scalar(bits[:, 0, :], edge_rows[:, 1, :], P - 1, None, ALU.bitwise_and)
            then(V.tensor_scalar(bits[:, 1, :], edge_rows[:, 1, :], P.bit_length() - 1, None, ALU.arith_shift_right))
            V.tensor_copy(key_rows[:, 0, :], bits[:, 0, :])
            V.tensor_scalar(key_rows[:, 1, :], bits[:, 1, :], float(WIN), None, ALU.mult)
            V.tensor_scalar(key_rows[:, 2, :], edge_rows[:, 0, :], group_lim[:, 0:1], None,
                            ALU.subtract).then_inc(rows_set, 1)
            dve.wait_ge(rows_turned, 1)
            then(V.tensor_copy(group_row[:].rearrange("p a g -> p (a g)"), bank[:, 0, 0:2 * G]))
            then(V.tensor_reduce(rounds_f[:, ROUNDS:ROUNDS + 1], group_row[:, 1, :], AX.X, ALU.max))
            then(V.tensor_scalar(rounds_f[:, 0:ROUNDS], span_at[:], rounds_f[:, ROUNDS:ROUNDS + 1], None, ALU.is_le))
            then(V.tensor_reduce(rounds_f[:, ROUNDS + 1:ROUNDS + 2], rounds_f[:, 0:ROUNDS], AX.X, ALU.add))
            then(V.tensor_copy(flags[0:1, 0:1], rounds_f[0:1, ROUNDS + 1:ROUNDS + 2]))
            V.memset(shift[:], 0.0).then_inc(rounds_set, 1)
            dve.wait_ge(rounds_set, 1)
            dve.wait_ge(rows_turned, 2)
            V.tensor_copy(edge_key[:, 0:2, :].rearrange("p a g -> p (a g)"), bank[:, 2, :]).then_inc(win_added, 1)
            V.tensor_copy(edge_key[:, 2, :], bank[:, 3, 0:CPG * G]).then_inc(win_added, 1)
            dve.wait_ge(win_added, 2)
            dve.wait_ge(const_set, 3)
            rounds = dve.value_load(flags[0:1, 0:1], min_val=1, max_val=ROUNDS)

            def one_hots(g, slot, chunks=range(CPG)):
                for c in chunks:
                    if c < BY_DVE:
                        V.tensor_scalar(hot_lo[:, slot * CPG + c, :], col_lo[:],
                                        edge_key[:, 0, bass.ds(g + c * G, 1)], None, ALU.is_equal)
                    V.tensor_scalar(hot_key[:, slot * CPG + c, :], col_key[:],
                                    keyed[:, 0, bass.ds(g + c * G, 1)], None, ALU.is_equal).then_inc(hot_set, 1)

            def windows_at(g):
                _, values = nc.values_load_multi_w_load_instructions(
                    base_at[0:1, bass.ds(g, BODY)], engines=[mybir.EngineType.DVE], min_val=0, max_val=N,
                    skip_runtime_bounds_check_because="the table's entries are clamped to [0, N] when it is written")
                return values

            def add_window(at_dst, seen, slot):
                dve.wait_ge(win_summed, seen + 1)
                dve.wait_ge(win_added, seen + 2)
                V.tensor_tensor(count[:, :, bass.ds(at_dst, WIN)],
                                bank[:, slot, 0:KEYS].rearrange("p (h d) -> p h d", h=NB),
                                count[:, :, bass.ds(at_dst, WIN)], ALU.add).then_inc(win_added, 1)

            SETUP = 8
            with dve.Fori(0, rounds) as r:
                def after(ins, n):
                    ins.then_inc(round_set, 1)
                    dve.wait_ge(round_set, r * SETUP + n)

                after(V.tensor_scalar(keyed[:, 1, :], edge_key[:, 2, :], shift[:], None, ALU.subtract), 1)
                after(V.tensor_scalar(keyed[:, 0, :], keyed[:, 1, :], 0.0, FAR, ALU.is_lt, ALU.mult), 2)
                after(V.tensor_scalar(keyed[:, 2, :], keyed[:, 1, :], float(WIN), FAR, ALU.is_ge, ALU.mult), 3)
                after(V.tensor_tensor(keyed[:, 0, :], keyed[:, 0, :], keyed[:, 2, :], ALU.add), 4)
                after(V.tensor_tensor(keyed[:, 0, :], keyed[:, 0, :], keyed[:, 1, :], ALU.add), 5)
                after(V.tensor_tensor(keyed[:, 0, :], keyed[:, 0, :], edge_key[:, 1, :], ALU.add), 6)
                after(V.tensor_scalar(base_at[:], group_row[0:1, 0, :], shift[0:1, :], float(N), ALU.add, ALU.min), 7)
                after(V.tensor_scalar(shift[:], shift[:], float(WIN), None, ALU.add), 8)
                one_hots(0, 0)
                with dve.Fori(0, G // BODY - 1) as q:
                    places = windows_at(q * BODY)
                    for n in range(BODY):
                        one_hots(q * BODY + (n + 1), (n + 1) % 2)
                        add_window(places[n], r * G + q * BODY + n, n % 2)
                places = windows_at(G - BODY)
                for n in range(G - BODY, G):
                    if n + 1 < G:
                        one_hots(n + 1, (n + 1) % 2)
                    add_window(places[n - (G - BODY)], r * G + n, n % 2)
            dve.wait_ge(win_added, rounds * G + 2)
            V.memset(rr[:], 0.0).then_inc(counted, 1)

            def low(n, y, of, scale):
                k = n % NB
                dve.wait_ge(hi_set, n + 1)
                V.scalar_tensor_tensor(out=y[1][:, k, :], in0=of, scalar=scale, in1=y[0][:, k, :].bitcast(F32),
                                       op0=ALU.mult, op1=ALU.subtract).then_inc(lo_set, 1)

            for h in range(NB):
                V.tensor_scalar(link[:, h, :], count[:, h, 0:N], 1.0, None, ALU.min).then_inc(link_set, 1)
            dve.wait_ge(unit_done, upto["u"])
            dve.wait_ge(link_set, NB)
            for h in range(NB):
                dve.wait_ge(link_turned, h + 1)
                V.scalar_tensor_tensor(out=sym[:, h, :], in0=bank[:, HALF + h % 3, :].bitcast(BF16), scalar=0.0,
                                       in1=link[:, h, :], op0=ALU.add, op1=ALU.max,
                                       accum_out=degs[:, 0, h:h + 1]).then_inc(sym_max, 1)
                if h >= 1:
                    low(h - 1, ya, xw[:, h - 1, :], dinv[:, 0, h - 1:h])
            low(NB - 1, ya, xw[:, NB - 1, :], dinv[:, 0, NB - 1:NB])

            def moments(n):
                j = n % NB
                then(V.bn_stats(stats[:], xs[:, j, :]))
                then(V.bn_aggr(mv[:, j, :], stats[:]))
                V.tensor_scalar(veps[:, j:j + 1], mv[:, j, 1:2], EPS, None, ALU.add).then_inc(var_set, 1)

            def residual(n, s, of_bias, scale):
                j, b = n % NB, n % HALF
                dve.wait_ge(hs_done, HALF * s + b + 1)
                dve.wait_ge(biased, of_bias + j + 1)
                V.scalar_tensor_tensor(out=xs[:, j, :], in0=bank[:, HALF * (s % 2) + b, :],
                                       scalar=dinv[:, scale, j:j + 1], in1=xs[:, j, :],
                                       op0=ALU.mult, op1=ALU.add).then_inc(dve_out, 1)
                dve.wait_ge(*freed(s, b))
                moments(n)

            def normalise(n):
                j = n % NB
                dve.wait_ge(rstd_set, n + 1)
                V.tensor_scalar(xs[:, j, :], xs[:, j, :], mv[:, j, 0:1], rstd[:, j:j + 1],
                                ALU.subtract, ALU.mult).then_inc(normed, 1)

            def make_rest(rest, turn):
                for h in range(NB):
                    own = slice(h * P, (h + 1) * P)
                    V.tensor_tensor(rest[:, h, :], count[:, h, 0:N], adj[:, h, :].bitcast(F32),
                                    ALU.subtract).then_inc(rest_part, 1)
                    dve.wait_ge(rest_part, turn * NB + h + 1)
                    ins = V.tensor_tensor(rest[:, h, own], rest[:, h, own].bitcast(F32), ident[:], ALU.add)
                ins.then_inc(rest_set, 1)

            def take_row(turn, first):
                dve.wait_ge(row_summed, turn + 1)
                V.tensor_copy(deg_row[0:1, :], bank[0:1, first:first + 2, :].rearrange("p a b -> p (a b)")
                              ).then_inc(row_out, 1)

            take_row(0, HALF + 2)
            residual(0, 0, 0, 0)
            dve.wait_ge(deg_summed, 1)
            V.tensor_copy(degs[:, 1, :], bank[:, 0, 0:NB]).then_inc(deg_out, 1)
            dve.wait_ge(deg_out, 1)
            V.tensor_reduce(degmax[:, 0:1], degs[:, 1, :], AX.X, ALU.max).then_inc(degmax_set, 1)
            for j in range(1, HALF):
                residual(j, 0, 0, 0)
                normalise(j - 1)
            normalise(HALF - 1)
            dve.wait_ge(degmax_all, 1)
            V.tensor_scalar(flags[0:1, 4:5], degmax[0:1, 1:2], float(EXACT), None, ALU.is_gt).then_inc(big_set, 1)
            dve.wait_ge(big_set, 1)
            big = dve.value_load(flags[0:1, 4:5], min_val=0, max_val=1)
            with dve.If(big > 0):
                dve.wait_ge(hs_done, 2 * HALF)
                make_rest(rest_l1, 0)
                take_row(1, 1)
                dve.wait_ge(deg_summed, 2)
                V.tensor_tensor(degs[:, 1, :], bank[:, 3, 0:NB], degs[:, 1, :], ALU.add).then_inc(deg_out, 1)
                dve.wait_ge(deg_out, 2)
            V.memset(degmax[:, 0:1], 0.0).then_inc(deg_set, 1)
            for j in range(HALF, NB):
                residual(j, 1, 0, 0)
                if j > HALF:
                    normalise(j - 1)
            normalise(NB - 1)

            dve.wait_ge(dinv_set, 1)
            for k in range(NB):
                low(NB + k, ya, bank[:, HALF + k % HALF, :], dinv[:, 1, k:k + 1])
            dve.wait_ge(unit_out, NU)
            for n, y, rows, fold in ((0, yb, rows_b, fold2), (1, ya, rows_a, fold1)):
                for k in range(NB + 1):
                    if k < NB:
                        dve.wait_ge(hs_done, (6 + 2 * n) * HALF + k + 1)
                        V.scalar_tensor_tensor(out=rows[:, k, :], in0=bank[:, k, :],
                                               scalar=dinv[:, 1, k:k + 1], in1=fold[:],
                                               op0=ALU.mult, op1=ALU.add).then_inc(dve_out, 1)
                    if k >= 1:
                        low((2 + n) * NB + k - 1, y, rows[:, k - 1, :], dinv[:, 1, k - 1:k])
            for j in range(NB):
                residual(NB + j, 10 + j // HALF, NB, 1)
                if j >= 1:
                    normalise(NB + j - 1)
            normalise(2 * NB - 1)

            V.tensor_reduce(c0[:, FB:FB + 1], c0[:, 0:FB], AX.X, ALU.add)
            for half in range(2):
                s = 13 + 3 * half
                for b in range(HALF):
                    j = HALF * half + b
                    dve.wait_ge(normed, NB + j + 1)
                    then(V.tensor_tensor_reduce(out=fold2[:], in0=xs[:, j, :], in1=urow[:], scale=1.0, scalar=0.0,
                                                op0=ALU.mult, op1=ALU.add, accum_out=rr[:, j:j + 1]))
                    V.tensor_scalar(rr[:, j:j + 1], rr[:, j:j + 1], c0[:, FB:FB + 1], None, ALU.add)
                for b in range(HALF):
                    j = HALF * half + b
                    dve.wait_ge(hs_done, HALF * s + b + 1)
                    V.tensor_tensor(vv[:, j, :], bank[:, HALF * (s % 2) + b, :], biasv[:], ALU.add).then_inc(dve_out, 1)
            dve.wait_ge(dve_out, freed(16, 3)[1])

            def mask_scores(i):
                dve.wait_ge(scored, i + 1)
                dve.wait_ge(masks_set, i + 1)
                if i >= 2:
                    dve.wait_ge(probs_turned, i - 1)
                V.scalar_tensor_tensor(out=score[:, i % 2, :],
                                       in0=bank[:, 2 * (i % 2):2 * (i % 2) + 2, :].rearrange("p a b -> p (a b)"),
                                       scalar=rr[:, i:i + 1], in1=mask[:, i % 2, :],
                                       op0=ALU.add, op1=ALU.mult).then_inc(score_out, 1)
                dve.wait_ge(score_out, i + 1)
                then(V.tensor_tensor_reduce(out=score[:, i % 2, :], in0=score[:, i % 2, :], in1=away[:, i % 2, :],
                                            scale=1.0, scalar=-3.0e38, op0=ALU.add, op1=ALU.max,
                                            accum_out=peak[:, 0, i:i + 1]))
                V.tensor_scalar(peak[:, 1, i:i + 1], peak[:, 0, i:i + 1], -1.0, None, ALU.mult).then_inc(peak_set, 1)

            def attended(i):
                dve.wait_ge(mixed, i + 1)
                dve.wait_ge(probs_set, i + 1)
                then(V.reciprocal(esum[:, 1, i:i + 1], esum[:, 0, i:i + 1]))
                V.scalar_tensor_tensor(out=xs[:, i, :], in0=bank[:, 6 + i % 2, :], scalar=esum[:, 1, i:i + 1],
                                       in1=xs[:, i, :], op0=ALU.mult, op1=ALU.add).then_inc(mixed_out, 1)
                dve.wait_ge(mixed_out, i + 1)
                moments(2 * NB + i)

            def low3(k):
                low(4 * NB + k, y3, xs[:, k, :], dinv[:, 1, k:k + 1])

            mask_scores(0)
            mask_scores(1)
            for i in range(NB):
                if i + 2 < NB:
                    mask_scores(i + 2)
                if i == NB - 3:
                    for k in range(EAGER):
                        low3(k)
                if i >= NB - 2:
                    low3(i - 2)
                attended(i)
                if i >= 1:
                    normalise(2 * NB + i - 1)
            normalise(3 * NB - 1)
            for k in range(NB - 2, NB):
                low3(k)

            with dve.If(big > 0):
                dve.wait_ge(mixed, NB)
                make_rest(rest_l3, 1)

            def hidden_low(k):
                dve.wait_ge(hi_set, 5 * NB + k + 1)
                then(V.tensor_scalar(hidden[:, k % 4, :], hidden[:, k % 4, :], dinv[:, 1, k:k + 1], 0.0,
                                     ALU.mult, ALU.max))
                V.tensor_tensor(y3[1][:, k, :], hidden[:, k % 4, :], y3[0][:, k, :].bitcast(F32),
                                ALU.subtract).then_inc(lo_set, 1)

            for k in range(NB):
                dve.wait_ge(hs_done, 20 * HALF + k + 1)
                V.scalar_tensor_tensor(out=hidden[:, k % 4, :], in0=bank[:, k, :], scalar=dinv[:, 1, k:k + 1],
                                       in1=biasc1[:], op0=ALU.mult, op1=ALU.add).then_inc(dve_out, 1)
                if k >= 1:
                    hidden_low(k - 1)
            hidden_low(NB - 1)
            for j in range(NB):
                residual(3 * NB + j, 24 + j // HALF, 2 * NB, 1)
                if j >= 1:
                    normalise(3 * NB + j - 1)
            normalise(4 * NB - 1)


_INS = ["x", "src", "dst", "L0_gnn_weight", "L0_gnn_bias", "L1_gnn_W1", "L1_gnn_b1", "L1_gnn_W2", "L1_gnn_b2",
        "L1_gnn_W3", "L1_gnn_b3", "L2_gnn_Wq", "L2_gnn_bq", "L2_gnn_Wk", "L2_gnn_bk", "L2_gnn_Wv", "L2_gnn_bv",
        "L3_gnn_W1", "L3_gnn_b1", "L3_gnn_W2", "L3_gnn_b2"]


def kernel(**inputs):
    import numpy as _np
    import concourse.bacc as _bacc
    from concourse import mybir as _mybir
    from concourse.bass_utils import run_bass_kernel_spmd as _run

    nc = _bacc.Bacc("TRN2", target_bir_lowering=False, num_devices=1)
    arrays, args = {}, []
    for name in _INS:
        a = _np.ascontiguousarray(inputs[name])
        arrays[f"in_{name}_dram"] = a
        args.append(nc.dram_tensor(f"in_{name}_dram", a.shape, _mybir.dt.from_np(a.dtype), kind="ExternalInput").ap())
    out = nc.dram_tensor("out_dram", inputs["x"].shape, _mybir.dt.float32, kind="ExternalOutput").ap()
    gnn_kernel(nc, *args, out)
    return _run(nc, [arrays], core_ids=[0]).results[0]["out_dram"]
```
